# Optimizing a Trainium2 kernel written in Bass

```python
import numpy as np
import jax
import jax.numpy as jnp

def _softmax(x, axis=-1):
    return jax.nn.softmax(x, axis=axis)

def _gelu(x):
    return jax.nn.gelu(x, approximate=True)

def _silu(x):
    return jax.nn.silu(x)

def _sigmoid(x):
    return jax.nn.sigmoid(x)

def _layernorm(x, axis=-1, eps=1e-05):
    m = jnp.mean(x, axis=axis, keepdims=True)
    v = jnp.var(x, axis=axis, keepdims=True)
    return (x - m) / jnp.sqrt(v + eps)

def _scatter_add(tgt, idx, src, axis=0):
    return tgt.at[idx].add(src)

def _segment_sum(src, seg, n):
    return jax.ops.segment_sum(src, seg, n)
kernel_name = 'mk_hybrid_d1_jaxref_r8_cbd4be'

def setup_inputs(seed: int=0):
    np.random.seed(seed)
    _w = jnp.asarray

    def _L0_attn_a_setup():
        import jax, jax.numpy as jnp
        import numpy as np
        D_MODEL = 128

        def bitlinear(x, weight):
            scale = jnp.clip(jnp.mean(jnp.abs(weight), axis=1, keepdims=True), 1e-05, None)
            w_q = jnp.clip(jnp.round(weight / scale), -1.0, 1.0)
            w = weight + jax.lax.stop_gradient(w_q * scale - weight)
            return x @ w.T

        def rmsnorm(x, w, eps=1e-06):
            return x * jax.lax.rsqrt(jnp.mean(x * x, axis=-1, keepdims=True) + eps) * w
        key = jax.random.key(seed)
        ks = jax.random.split(key, 6)
        D = D_MODEL
        std = np.sqrt(2.0 / D)
        return {'x': jax.random.normal(ks[0], (4, 512, D), dtype=jnp.float32), 'Wr': jax.random.normal(ks[1], (D, D), dtype=jnp.float32) * std, 'Wk': jax.random.normal(ks[2], (D, D), dtype=jnp.float32) * std, 'Wv': jax.random.normal(ks[3], (D, D), dtype=jnp.float32) * std, 'Wo': jax.random.normal(ks[4], (D, D), dtype=jnp.float32) * std, 'decay': jnp.ones((D,), dtype=jnp.float32) * 0.99, 'ln_w': jnp.ones((D,), dtype=jnp.float32)}
    _L0_attn_a_in = _L0_attn_a_setup()

    def _L0_attn_b_setup():
        import jax, jax.numpy as jnp
        import numpy as np
        DIM = 128
        NUM_HEADS = 16
        HEAD_DIM = DIM // NUM_HEADS
        B, L = (4, 256)

        def _alibi_bias_causal(seq_len, dtype):
            h = jnp.arange(1, NUM_HEADS + 1, dtype=jnp.float32)
            slopes = jnp.power(2.0, -8.0 * h / NUM_HEADS)
            pos = jnp.arange(seq_len, dtype=jnp.float32)
            rel = jnp.abs(pos[:, None] - pos[None, :])
            bias = -slopes[:, None, None] * rel[None, :, :]
            causal = pos[:, None] >= pos[None, :]
            bias = jnp.where(causal[None, :, :], bias, -jnp.inf)
            return bias.astype(dtype)
        key = jax.random.key(seed)
        ks = jax.random.split(key, 9)
        s = 0.02
        return {'x': jax.random.normal(ks[0], (B, L, DIM), jnp.float32), 'Wq': jax.random.normal(ks[1], (DIM, DIM), jnp.float32) * s, 'bq': jax.random.normal(ks[2], (DIM,), jnp.float32) * s, 'Wk': jax.random.normal(ks[3], (DIM, DIM), jnp.float32) * s, 'bk': jax.random.normal(ks[4], (DIM,), jnp.float32) * s, 'Wv': jax.random.normal(ks[5], (DIM, DIM), jnp.float32) * s, 'bv': jax.random.normal(ks[6], (DIM,), jnp.float32) * s, 'Wo': jax.random.normal(ks[7], (DIM, DIM), jnp.float32) * s, 'bo': jax.random.normal(ks[8], (DIM,), jnp.float32) * s}
    _L0_attn_b_in = _L0_attn_b_setup()

    def _L0_ffn_setup():
        import jax, jax.numpy as jnp
        import numpy as np
        DIM = 128

        def _reference_tuple_inner(x, W_r, W_k, W_v, mu_r, mu_k):
            B, T, C = x.shape
            x_prev = jnp.concatenate([jnp.zeros((B, 1, C), x.dtype), x[:, :-1, :]], axis=1)
            xr = mu_r * x + (1.0 - mu_r) * x_prev
            xk = mu_k * x + (1.0 - mu_k) * x_prev
            r = jax.nn.sigmoid(jnp.einsum('btc,dc->btd', xr, W_r))
            k = jnp.einsum('btc,dc->btd', xk, W_k)
            k_act = jnp.square(jax.nn.relu(k))
            out = r * jnp.einsum('btc,dc->btd', k_act, W_v)
            new_state = x[:, -1, :]
            return (out, new_state)
        key = jax.random.key(seed)
        ks = jax.random.split(key, 6)
        B, T, C = (8, 256, DIM)
        x = jax.random.normal(ks[0], (B, T, C), dtype=jnp.float32)
        s = 1.0 / np.sqrt(C)
        W_r = jax.random.uniform(ks[1], (C, C), jnp.float32, -s, s)
        W_k = jax.random.uniform(ks[2], (C, C), jnp.float32, -s, s)
        W_v = jax.random.uniform(ks[3], (C, C), jnp.float32, -s, s)
        mu_r = jax.random.uniform(ks[4], (C,), jnp.float32)
        mu_k = jax.random.uniform(ks[5], (C,), jnp.float32)
        return {'x': x, 'W_r': W_r, 'W_k': W_k, 'W_v': W_v, 'mu_r': mu_r, 'mu_k': mu_k}
    _L0_ffn_in = _L0_ffn_setup()
    _d = {'L0_attn_a_x': _L0_attn_a_in['x'], 'L0_attn_a_Wr': _L0_attn_a_in['Wr'], 'L0_attn_a_Wk': _L0_attn_a_in['Wk'], 'L0_attn_a_Wv': _L0_attn_a_in['Wv'], 'L0_attn_a_Wo': _L0_attn_a_in['Wo'], 'L0_attn_a_decay': _L0_attn_a_in['decay'], 'L0_attn_a_ln_w': _L0_attn_a_in['ln_w'], 'L0_attn_b_Wq': _L0_attn_b_in['Wq'], 'L0_attn_b_bq': _L0_attn_b_in['bq'], 'L0_attn_b_Wk': _L0_attn_b_in['Wk'], 'L0_attn_b_bk': _L0_attn_b_in['bk'], 'L0_attn_b_Wv': _L0_attn_b_in['Wv'], 'L0_attn_b_bv': _L0_attn_b_in['bv'], 'L0_attn_b_Wo': _L0_attn_b_in['Wo'], 'L0_attn_b_bo': _L0_attn_b_in['bo'], 'L0_ffn_W_r': _L0_ffn_in['W_r'], 'L0_ffn_W_k': _L0_ffn_in['W_k'], 'L0_ffn_W_v': _L0_ffn_in['W_v'], 'L0_ffn_mu_r': _L0_ffn_in['mu_r'], 'L0_ffn_mu_k': _L0_ffn_in['mu_k']}
    _x0 = _d['L0_attn_a_x']
    _d['L0_attn_a_x'] = jax.random.normal(jax.random.fold_in(jax.random.key(seed), 1), (8, 512, 128), dtype=_x0.dtype)
    del _x0
    return _d

def reference(L0_attn_a_x, L0_attn_a_Wr, L0_attn_a_Wk, L0_attn_a_Wv, L0_attn_a_Wo, L0_attn_a_decay, L0_attn_a_ln_w, L0_attn_b_Wq, L0_attn_b_bq, L0_attn_b_Wk, L0_attn_b_bk, L0_attn_b_Wv, L0_attn_b_bv, L0_attn_b_Wo, L0_attn_b_bo, L0_ffn_W_r, L0_ffn_W_k, L0_ffn_W_v, L0_ffn_mu_r, L0_ffn_mu_k):

    def _L0_attn_a_ref(x, Wr, Wk, Wv, Wo, decay, ln_w):
        import jax, jax.numpy as jnp
        import numpy as np
        D_MODEL = 128

        def bitlinear(x, weight):
            scale = jnp.clip(jnp.mean(jnp.abs(weight), axis=1, keepdims=True), 1e-05, None)
            w_q = jnp.clip(jnp.round(weight / scale), -1.0, 1.0)
            w = weight + jax.lax.stop_gradient(w_q * scale - weight)
            return x @ w.T

        def rmsnorm(x, w, eps=1e-06):
            return x * jax.lax.rsqrt(jnp.mean(x * x, axis=-1, keepdims=True) + eps) * w
        B, T, D = x.shape
        r = jax.nn.sigmoid(bitlinear(x, Wr))
        k = bitlinear(x, Wk)
        v = bitlinear(x, Wv)
        dec = jax.nn.sigmoid(decay)
        kv = k * v
        positions = jnp.arange(T, dtype=x.dtype)
        log_decay = jnp.log(jnp.clip(dec, 1e-07, None))
        scale = jnp.exp(positions[:, None] * log_decay[None, :])
        scaled = kv / jnp.clip(scale, 1e-10, None)[None]
        cum = jnp.cumsum(scaled, axis=1)
        state = cum * scale[None]
        return bitlinear(rmsnorm(r * state, ln_w), Wo)

    def _L0_attn_b_ref(x, Wq, bq, Wk, bk, Wv, bv, Wo, bo):
        import jax, jax.numpy as jnp
        import numpy as np
        DIM = 128
        NUM_HEADS = 16
        HEAD_DIM = DIM // NUM_HEADS
        B, L = (4, 256)

        def _alibi_bias_causal(seq_len, dtype):
            h = jnp.arange(1, NUM_HEADS + 1, dtype=jnp.float32)
            slopes = jnp.power(2.0, -8.0 * h / NUM_HEADS)
            pos = jnp.arange(seq_len, dtype=jnp.float32)
            rel = jnp.abs(pos[:, None] - pos[None, :])
            bias = -slopes[:, None, None] * rel[None, :, :]
            causal = pos[:, None] >= pos[None, :]
            bias = jnp.where(causal[None, :, :], bias, -jnp.inf)
            return bias.astype(dtype)
        b, l, d = x.shape
        q = (jnp.einsum('bld,ed->ble', x, Wq) + bq).reshape(b, l, NUM_HEADS, HEAD_DIM).transpose(0, 2, 1, 3)
        k = (jnp.einsum('bld,ed->ble', x, Wk) + bk).reshape(b, l, NUM_HEADS, HEAD_DIM).transpose(0, 2, 1, 3)
        v = (jnp.einsum('bld,ed->ble', x, Wv) + bv).reshape(b, l, NUM_HEADS, HEAD_DIM).transpose(0, 2, 1, 3)
        scale = 1.0 / np.sqrt(HEAD_DIM)
        scores = jnp.einsum('bhqd,bhkd->bhqk', q, k) * scale
        scores = scores + _alibi_bias_causal(l, scores.dtype)[None]
        attn = jax.nn.softmax(scores, axis=-1)
        out = jnp.einsum('bhqk,bhkd->bhqd', attn, v)
        out = out.transpose(0, 2, 1, 3).reshape(b, l, d)
        return jnp.einsum('bld,ed->ble', out, Wo) + bo

    def _L0_ffn_ref(x, W_r, W_k, W_v, mu_r, mu_k):
        import jax, jax.numpy as jnp
        import numpy as np
        DIM = 128

        def _reference_tuple_inner(x, W_r, W_k, W_v, mu_r, mu_k):
            B, T, C = x.shape
            x_prev = jnp.concatenate([jnp.zeros((B, 1, C), x.dtype), x[:, :-1, :]], axis=1)
            xr = mu_r * x + (1.0 - mu_r) * x_prev
            xk = mu_k * x + (1.0 - mu_k) * x_prev
            r = jax.nn.sigmoid(jnp.einsum('btc,dc->btd', xr, W_r))
            k = jnp.einsum('btc,dc->btd', xk, W_k)
            k_act = jnp.square(jax.nn.relu(k))
            out = r * jnp.einsum('btc,dc->btd', k_act, W_v)
            new_state = x[:, -1, :]
            return (out, new_state)
        return _reference_tuple_inner(x, W_r, W_k, W_v, mu_r, mu_k)[0]
    x = L0_attn_a_x
    x = x + _L0_attn_a_ref(_layernorm(x, axis=-1), L0_attn_a_Wr, L0_attn_a_Wk, L0_attn_a_Wv, L0_attn_a_Wo, L0_attn_a_decay, L0_attn_a_ln_w)
    x = x + _L0_ffn_ref(_layernorm(x, axis=-1), L0_ffn_W_r, L0_ffn_W_k, L0_ffn_W_v, L0_ffn_mu_r, L0_ffn_mu_k)
    x = x + _L0_attn_b_ref(_layernorm(x, axis=-1), L0_attn_b_Wq, L0_attn_b_bq, L0_attn_b_Wk, L0_attn_b_bk, L0_attn_b_Wv, L0_attn_b_bv, L0_attn_b_Wo, L0_attn_b_bo)
    x = x + _L0_ffn_ref(_layernorm(x, axis=-1), L0_ffn_W_r, L0_ffn_W_k, L0_ffn_W_v, L0_ffn_mu_r, L0_ffn_mu_k)
    return x

_drawn_inputs = setup_inputs


def setup_inputs(seed=0):
    import zlib

    import numpy as np

    out = dict(_drawn_inputs(seed))
    spreads = {'L0_attn_a_decay': (0.9900000095367432, 0.2), 'L0_attn_a_ln_w': (1.0, 0.2)}
    factors = {'L0_attn_b_Wq': 8.0,
     'L0_attn_b_bq': 8.0,
     'L0_attn_b_Wk': 8.0,
     'L0_attn_b_bk': 8.0,
     'L0_attn_b_Wv': 3.525,
     'L0_attn_b_bv': 8.0,
     'L0_attn_b_Wo': 3.392,
     'L0_attn_b_bo': 3.115,
     'L0_ffn_mu_r': 3.698}
    for name, (base, spread) in spreads.items():
        noise = np.random.default_rng([zlib.crc32(name.encode()), seed]).standard_normal(out[name].shape)
        drawn = base * np.exp(spread * noise) if base else spread * noise
        out[name] = jnp.asarray(drawn.astype(out[name].dtype))
    for name, factor in factors.items():
        out[name] = (out[name] * factor).astype(out[name].dtype)
    return out
```

```python
from contextlib import ExitStack

import numpy as np

import concourse.bass as bass
from concourse import mybir

F32 = mybir.dt.float32
BF16 = mybir.dt.bfloat16
ACT = mybir.ActivationFunctionType
ALU = mybir.AluOpType
AX = mybir.AxisListType

P = 128
B = 8
T = 512
NT = T // P
D = 128
H = 16
HD = D // H
G = 4
NG = H // G
VW = 32
SCALE = 1.0 / np.sqrt(HD)
LN_EPS = 1e-5
RMS_EPS = 1e-6
CLIP_SCALE = 1e-10

SUB = 16
NBIAS = 12
NCONST = NBIAS + T // SUB - 1
FAR = -1e30
NSPLIT = 6 * HD
MROW = 96
KROWS = MROW + 2

WIDTH = [T - P * j for j in range(NT)]
PT_AT = [G * sum(WIDTH[:j]) for j in range(NT)]
PT_COLS = G * sum(WIDTH)

P1_UNITS = [[(h, 3)] for h in range(G)] + [[(0, 1), (1, 1)], [(2, 1), (3, 1)]] + [[(h, 2), (h, 0)] for h in range(G)]
P2_UNITS = [(0, [h]) for h in range(G)] + [(1, [h]) for h in range(G)] + [(2, [0, 1]), (2, [2, 3]), (3, [0, 1, 2, 3])]
N1, N2 = len(P1_UNITS) + 1, len(P2_UNITS)
STEPS = 11
EXPS_OF = [sum(1 for j, _ in P2_UNITS if j <= jj) for jj in range(NT)]
LAG = 4
PV_STEP = {2: 0, 3: 1, 5: 2, 7: 3}


def build(nc, x, w_a, w_f, w_b, decay, ln_w, mu, b_cols, bo_row, ident, ident_b, causal, pos, aug_q, aug_k, out):
    ctx = ExitStack()
    with ctx:
        def sb(name, shape, dt=F32):
            return ctx.enter_context(nc.sbuf_tensor(name, shape, dt))

        def ps(name):
            return ctx.enter_context(nc.psum_tensor(name, [P, T], F32))

        def sem(name):
            return ctx.enter_context(nc.semaphore(name))

        s1_bank = [ps("s1_bank0"), ps("s1_bank1")]
        s2_bank = [ps("s2_bank0"), ps("s2_bank1")]
        o_bank = ps("o_bank")
        a_bank = ps("a_bank")
        b_bank = ps("b_bank")
        c_bank = ps("c_bank")

        id_f = sb("id_f", [P, P])
        id_b = sb("id_b", [P, P], BF16)
        mask_b = sb("mask_b", [P, P], BF16)
        w_table = sb("w_table", [P, T])
        bsum = sb("bsum", [P, 4])
        bscale = sb("bscale", [P, 4])
        bhalf = sb("bhalf", [P, 2, 4])
        wa = sb("wa", [P, 4, P])
        wf = sb("wf", [P, 3, P])
        wb = sb("wb", [P, 4, P])
        dcol = sb("dcol", [P, 6])
        lnw = sb("lnw", [P, 1])
        mu_sb = sb("mu_sb", [P, 2])
        bcol = sb("bcol", [P, 3])
        bq_s = sb("bq_s", [P, 1])
        ones_f = sb("ones_f", [P, P])
        bv_b = sb("bv_b", [P, P])
        bo_b = sb("bo_b", [P, P])
        bias_o = sb("bias_o", [P, P])
        neg_half = sb("neg_half", [P, NT])

        x_in = [sb(f"x_in{p}", [P, NT, D]) for p in range(2)]
        x_1 = [sb("x_1", [P, NT, D])] * 2
        x_2 = [sb(f"x_2{p}", [P, NT, D]) for p in range(2)]
        x_2b = sb("x_2b", [P, NT, D])
        x_3 = [sb("x_3", [P, NT, D])] * 2
        LN = ["retention", "ffn1", "attention", "ffn2"]
        st = {k: sb(f"st_{k}", [P, NT, 6]) for k in LN}
        mv = {k: sb(f"mv_{k}", [P, NT, 2]) for k in LN}
        ve = {k: sb(f"ve_{k}", [P, NT]) for k in LN}
        rstd = {k: sb(f"rstd_{k}", [P, NT]) for k in LN}
        nmean = {k: sb(f"nmean_{k}", [P, NT]) for k in LN}
        xn = {k: sb(f"xn_{k}", [P, NT, D]) for k in LN[1:]}
        xnt = {k: sb(f"xnt_{k}", [P, 1 + T]) for k in LN[1:]}
        xn["retention"], xnt["retention"] = xn["ffn1"], xnt["ffn1"]

        k_sb = sb("k_sb", [P, T])
        kw = sb("kw", [P, T])
        kvw = sb("kvw", [P, T])
        state = k_sb
        r_tanh = sb("r_tanh", [P, T])
        u = kvw
        usq = kw
        msq = sb("msq", [P, NT])
        rrms = sb("rrms", [P, NT])

        FF = ["ffn1", "ffn2"]
        dx = {k: sb(f"dx_{k}", [P, T]) for k in FF}
        xr = {k: sb(f"xr_{k}", [P, T]) for k in FF}
        xk = {k: sb(f"xk_{k}", [P, T]) for k in FF}
        f_tanh = {k: sb(f"f_tanh_{k}", [P, T]) for k in FF}
        k_relu = {k: sb(f"k_relu_{k}", [P, T]) for k in FF}
        k_act = k_relu
        gated = dx
        x_out = dx["ffn2"][:].rearrange("p (t d) -> p t d", t=NT)

        qf = {n: sb(f"{n}f", [P, T]) for n in "qk"}
        qres = {n: sb(f"{n}res", [P, T]) for n in "qk"}
        parts = {n: sb(f"{n}parts", [P, 3, T], BF16) for n in "qk"}
        q_aug = [sb(f"q_aug{p}", [P, H, T], BF16) for p in range(2)]
        k_aug = [sb(f"k_aug{p}", [P, H, T], BF16) for p in range(2)]
        v_aug = [sb(f"v_aug{p}", [P, NT, H, VW]) for p in range(2)]
        q_dram = [nc.dram_tensor(f"q_dram{p}", [H, 3, HD, T], BF16, kind="Internal").ap() for p in range(2)]
        k_dram = [nc.dram_tensor(f"k_dram{p}", [H, 3, HD, T], BF16, kind="Internal").ap() for p in range(2)]

        bmax = [sb(f"bmax{p}", [P, G, NT]) for p in range(2)]
        negm = [sb(f"negm{p}", [P, G, NT]) for p in range(2)]
        m_parts = [sb(f"m_parts{p}", [P, 2, G * NT], BF16) for p in range(2)]
        m_rows = [sb(f"m_rows{p}", [2 * G * NT, P], BF16) for p in range(2)]
        pt = [sb(f"pt{p}", [P, PT_COLS]) for p in range(2)]
        bw = pt[1][:, 0:4 * P].rearrange("p (w c) -> p w c", w=4)
        bw_q = pt[1][:, 4 * P:8 * P].rearrange("p (w c) -> p w c", w=4)
        bw_gt = pt[1][:, 8 * P:9 * P]
        bw_lt = pt[1][:, 9 * P:10 * P]
        o_sb = [sb("o_sb", [P, T])] * 2
        rsum = sb("rsum", [P, NT, G])
        o_tm = [sb("o_tm", [P, NT, D])] * 2
        o_t = xr["ffn2"]

        consts_in = sem("consts_in")
        weights_in = sem("weights_in")
        aug_in = sem("aug_in")
        zeroed = sem("zeroed")
        pool_set = sem("pool_set")
        dve_set = sem("dve_set")
        act_set = sem("act_set")
        pe_set = sem("pe_set")
        bw_set = sem("bw_set")
        x_loaded = [sem(f"x_loaded{p}") for p in range(2)]
        stored = [sem(f"stored{p}") for p in range(2)]
        stats = {k: sem(f"stats_{k}") for k in LN}
        norm = {k: sem(f"norm_{k}") for k in LN}
        turned = {k: sem(f"turned_{k}") for k in LN}
        xt_ready = {k: sem(f"xt_{k}") for k in LN}
        a_k, a_r, a_v, a_ss, a_y = (sem(n) for n in ("a_k", "a_r", "a_v", "a_ss", "a_y"))
        k_copied, a_tanh, kw_ready, usq_ready, rrms_ready = (
            sem(n) for n in ("k_copied", "a_tanh", "kw_ready", "usq_ready", "rrms_ready"))
        scan_steps = sem("scan_steps")
        msq_ready = sem("msq_ready")
        x1_ready = sem("x1_ready")
        dx_ready = {k: sem(f"dx_{k}_ready") for k in FF}
        mixed = {k: sem(f"mixed_{k}") for k in FF}
        f_r = {k: sem(f"f_r_{k}") for k in FF}
        f_k = {k: sem(f"f_k_{k}") for k in FF}
        f_v = {k: sem(f"f_v_{k}") for k in FF}
        f_tanh_ready = {k: sem(f"f_tanh_ready_{k}") for k in FF}
        relu_ready = {k: sem(f"relu_ready_{k}") for k in FF}
        act_ready = {k: sem(f"act_ready_{k}") for k in FF}
        gated_ready = {k: sem(f"gated_ready_{k}") for k in FF}
        ffn_out = {k: sem(f"ffn_out_{k}") for k in FF}
        x2b_ready = sem("x2b_ready")
        b_q, b_k, b_v = sem("b_q"), sem("b_k"), sem("b_v")
        qf_ready = {n: sem(f"{n}f_ready") for n in "qk"}
        cast = {n: sem(f"{n}_cast") for n in "qk"}
        rest = {n: sem(f"{n}_rest") for n in "qk"}
        v_ready = sem("v_ready")
        parts_out = [sem(f"parts_out{p}") for p in range(2)]
        aug_loaded = [sem(f"aug_loaded{p}") for p in range(2)]
        s1_full, s1_free = sem("s1_full"), sem("s1_free")
        negm_ready = sem("negm_ready")
        mparts_ready = sem("mparts_ready")
        m_loaded = [sem(f"m_loaded{p}") for p in range(2)]
        s2_full, exp_done = sem("s2_full"), sem("exp_done")
        masked, pv_done = sem("masked"), sem("pv_done")
        o_copied, o_turned = sem("o_copied"), sem("o_turned")
        o_normed = sem("o_normed")
        c_turned, ot_ready, c_y, x3_ready = sem("c_turned"), sem("ot_ready"), sem("c_y"), sem("x3_ready")

        BANK = {"retention": a_bank, "ffn1": a_bank, "attention": b_bank, "ffn2": c_bank}
        SRC = {"retention": x_in, "ffn1": x_1, "attention": x_2, "ffn2": x_3}
        DST = {"ffn1": x_2, "ffn2": [x_out, x_out]}

        def reach(eng, s, b, k=1, n=1):
            v = n * b + k
            if isinstance(v, int) and v <= 0:
                return
            eng.wait_ge(s, v)

        def wait_source(eng, k, b, p):
            if k == "retention":
                eng.wait_ge(x_loaded[p], 16 * (b // 2 + 1))
            elif k == "ffn1":
                reach(eng, x1_ready, b)
            elif k == "attention":
                reach(eng, ffn_out["ffn1"], b)
            else:
                reach(eng, x3_ready, b)

        block = ctx.enter_context(nc.Block())

        ITERATIONS = range(-2, B + 1)

        def has(b, lo=0, hi=B):
            return lo <= b < hi

        def slots(b):
            for at in range(NG * STEPS):
                g, k = divmod(at, STEPS)
                yield at, NG * b + g, g, k

        def live(s):
            return 0 <= s < NG * B

        DVE_TABLE, DVE_BIAS, DVE_ALL = 5, 10, 10

        @block.sync
        def _(sp):
            sp.dma_start(bw, w_a).then_inc(weights_in, 16)
            sp.dma_start(id_f[:], ident).then_inc(consts_in, 16)
            sp.dma_start(x_in[0][:], x[0].rearrange("(t p) d -> p t d", p=P)).then_inc(x_loaded[0], 16)
            sp.dma_start(w_table[:], pos).then_inc(consts_in, 16)
            sp.dma_start(dcol[:, 0:1], decay).then_inc(consts_in, 16)
            sp.dma_start(lnw[:], ln_w).then_inc(consts_in, 16)
            sp.dma_start(mu_sb[:], mu).then_inc(consts_in, 16)
            sp.dma_start(bcol[:], b_cols).then_inc(consts_in, 16)
            sp.dma_start(bo_b[:], bo_row.to_broadcast([P, D])).then_inc(consts_in, 16)
            sp.dma_start(wf[:], w_f).then_inc(weights_in, 16)
            sp.dma_start(wb[:], w_b).then_inc(weights_in, 16)
            sp.dma_start(x_in[1][:], x[1].rearrange("(t p) d -> p t d", p=P)).then_inc(x_loaded[1], 16)
            sp.dma_start(id_b[:], ident_b).then_inc(consts_in, 16)
            sp.dma_start(mask_b[:], causal).then_inc(consts_in, 16)
            sp.wait_ge(zeroed, 4)
            for p in range(2):
                sp.dma_start(q_aug[p][0:NCONST], aug_q).then_inc(aug_in, 16)
                sp.dma_start(k_aug[p][0:NCONST], aug_k).then_inc(aug_in, 16)

            def m_rows_in(s, g, b):
                p = s % 2
                reach(sp, s1_free, b, N1 * g + 10 + 1, NG * N1)
                dst = q_aug[(s // NG) % 2]
                for r in range(2):
                    sp.dma_start(dst[MROW + r:MROW + r + 1, G * g:G * g + G, :]
                                 .rearrange("o h (i q) -> o (h i) q", q=P),
                                 m_rows[p][G * NT * r:G * NT * (r + 1), :]).then_inc(m_loaded[p], 16)

            def parts_to_dram(b, n):
                p = b % 2
                reach(sp, rest[n], b, 2, 2)
                dram = (q_dram if n == "q" else k_dram)[p]
                for i in range(3):
                    sp.dma_start(dram[:, i], parts[n][:, i, :]).then_inc(parts_out[p], 16)

            def parts_to_rows(b):
                p = b % 2
                sp.wait_ge(parts_out[p], 96 * (b // 2 + 1))
                reach(sp, s2_full, b - 2, NG * N2, NG * N2)
                row = NCONST
                for reps in (3, 2, 1):
                    sp.dma_start(q_aug[p][row:row + HD * reps],
                                 q_dram[p][:, 0:reps].rearrange("h s d t -> (s d) h t")).then_inc(aug_loaded[p], 16)
                    for _ in range(reps):
                        sp.dma_start(k_aug[p][row:row + HD],
                                     k_dram[p][:, 3 - reps].rearrange("h d t -> d h t")).then_inc(aug_loaded[p], 16)
                        row += HD

            def iteration(b):
                for at, s, g, k in slots(b):
                    if k == 1 and live(s):
                        m_rows_in(s, g, b)
                    if at == 24 and has(b + 1):
                        parts_to_dram(b + 1, "q")
                    if at == 26 and has(b + 1):
                        parts_to_dram(b + 1, "k")
                        parts_to_rows(b + 1)
                    if at == 30 and has(b + 4, 2):
                        reach(sp, x1_ready, b + 2)
                        sp.dma_start(x_in[b % 2][:], x[b + 4].rearrange("(t p) d -> p t d", p=P))\
                          .then_inc(x_loaded[b % 2], 16)
                    if at == 43 and has(b - 1):
                        reach(sp, ffn_out["ffn2"], b - 1)
                        sp.dma_start(out[b - 1].rearrange("(t p) d -> p t d", p=P), x_out)\
                          .then_inc(stored[(b - 1) % 2], 16)

            for b in ITERATIONS:
                iteration(b)
            for p in range(2):
                sp.wait_ge(stored[p], 16 * (B // 2))

        @block.gpsimd
        def _(pool):
            pool.memset(neg_half[:], -0.5).then_inc(pool_set, 1)
            for k in FF:
                pool.memset(xnt[k][:, 0:1], 0.0).then_inc(pool_set, 1)
            pool.memset(ones_f[:], 1.0).then_inc(pool_set, 1)
            pool.memset(q_aug[0][:], 0.0).then_inc(zeroed, 1)
            pool.memset(q_aug[1][:], 0.0).then_inc(zeroed, 1)
            for p in range(2):
                pool.memset(v_aug[p][:], 1.0).then_inc(pool_set, 1)

            def normalise(k, b):
                p = b % 2
                reach(pool, stats[k], b, 2, 2)
                pool.tensor_scalar(ve[k][:], mv[k][:, :, 1], 1.0, LN_EPS, ALU.mult, ALU.add).then_inc(norm[k], 1)
                pool.tensor_scalar(nmean[k][:], mv[k][:, :, 0], -1.0, 0.0, ALU.mult, ALU.add).then_inc(norm[k], 1)
                reach(pool, norm[k], b, 2, 4)
                pool.tensor_tensor(rstd[k][:], ve[k][:], neg_half[:], ALU.pow).then_inc(norm[k], 1)
                reach(pool, norm[k], b, 3, 4)
                reach(pool, turned[k], b - 1)
                for t in range(NT):
                    last = pool.tensor_scalar(xn[k][:, t, :], SRC[k][p][:, t, :], nmean[k][:, t:t + 1],
                                              rstd[k][:, t:t + 1], ALU.add, ALU.mult)
                last.then_inc(norm[k], 1)

            def key_times_table(b):
                reach(pool, k_copied, b)
                reach(pool, scan_steps, b - 1, 1, 3)
                if b == 0:
                    pool.wait_ge(dve_set, DVE_TABLE)
                pool.tensor_tensor(kw[:], k_sb[:], w_table[:], ALU.mult).then_inc(kw_ready, 1)

            def square_u(b):
                reach(pool, scan_steps, b, 3, 3)
                reach(pool, a_ss, b - 1)
                pool.tensor_tensor(usq[:], u[:], u[:], ALU.mult).then_inc(usq_ready, 1)

            def rms_power(b):
                reach(pool, msq_ready, b)
                reach(pool, x1_ready, b - 1)
                pool.tensor_tensor(rrms[:], msq[:], neg_half[:], ALU.pow).then_inc(rrms_ready, 1)

            def token_difference(k, b):
                reach(pool, xt_ready[k], b)
                reach(pool, mixed[k], b - 1, 2, 2)
                if k == "ffn2" and b >= 1:
                    pool.wait_ge(stored[(b - 1) % 2], 16 * ((b - 1) // 2 + 1))
                pool.tensor_tensor(dx[k][:], xnt[k][:, 1:1 + T], xnt[k][:, 0:T], ALU.subtract)\
                    .then_inc(dx_ready[k], 1)

            def square_relu(k, b):
                reach(pool, relu_ready[k], b)
                reach(pool, f_v[k], b - 1)
                pool.tensor_tensor(k_act[k][:], k_relu[k][:], k_relu[k][:], ALU.mult).then_inc(act_ready[k], 1)

            def ffn_residual(k, b):
                p = b % 2
                reach(pool, gated_ready[k], b)
                pool.tensor_tensor(DST[k][p][:], gated[k][:].rearrange("p (t d) -> p t d", t=NT),
                                   SRC[k][p][:], ALU.add).then_inc(ffn_out[k], 1)

            def residual_bias(b):
                p = b % 2
                reach(pool, x3_ready, b - 1)
                if b == 0:
                    pool.wait_ge(dve_set, DVE_BIAS)
                pool.tensor_tensor(x_2b[:], x_2[p][:],
                                   bias_o[:].rearrange("p (o d) -> p o d", o=1).to_broadcast([P, NT, D]),
                                   ALU.add).then_inc(x2b_ready, 1)

            def split_rest(n, b, i):
                reach(pool, cast[n], b, i + 1, 2)
                if i == 0:
                    pool.tensor_tensor(qres[n][:], qf[n][:], parts[n][:, 0, :], ALU.subtract).then_inc(rest[n], 1)
                else:
                    pool.tensor_tensor(parts[n][:, 2, :], qres[n][:], parts[n][:, 1, :], ALU.subtract)\
                        .then_inc(rest[n], 1)

            def split_max(s, b, g):
                p = s % 2
                reach(pool, negm_ready, b, 2 * g + 2, 2 * NG)
                pool.tensor_copy(m_parts[p][:, 0, :], negm[p][:].rearrange("p h i -> p (h i)"))\
                    .then_inc(mparts_ready, 1)
                reach(pool, mparts_ready, b, 2 * g + 1, 2 * NG)
                pool.tensor_tensor(m_parts[p][:, 1, :], negm[p][:].rearrange("p h i -> p (h i)"),
                                   m_parts[p][:, 0, :], ALU.subtract).then_inc(mparts_ready, 1)

            def mask_diagonal(s, b, g, j):
                reach(pool, exp_done, b, N2 * g + EXPS_OF[j], NG * N2)
                blk = pt[s % 2][:, PT_AT[j]:PT_AT[j] + G * WIDTH[j]].rearrange("p (h q) -> p h q", h=G)[:, :, 0:P]
                pool.affine_select(out=blk, in_=blk, compare_op=ALU.is_ge, fill=0.0, base=0,
                                   pattern=[[0, G], [1, P]], channel_multiplier=-1).then_inc(masked, 1)

            def iteration(b):
                for at, s, g, k in slots(b):
                    if k == 0 and live(s):
                        split_max(s, b, g)
                    for j, (slot_before, step) in enumerate([(0, 9), (1, 1), (1, 4), (1, 5)]):
                        if k == step and live(s - slot_before):
                            bb, gg = (b, g - slot_before) if g >= slot_before else (b - 1, g - slot_before + NG)
                            mask_diagonal(s - slot_before, bb, gg, j)
                    if has(b) and at == 20:
                        residual_bias(b)
                    if has(b + 2):
                        if at == 2:
                            normalise("retention", b + 2)
                        if at == 8:
                            key_times_table(b + 2)
                        if at == 14:
                            square_u(b + 2)
                        if at == 18:
                            rms_power(b + 2)
                        if at == 22:
                            normalise("ffn1", b + 2)
                        if at == 26:
                            token_difference("ffn1", b + 2)
                        if at == 33:
                            square_relu("ffn1", b + 2)
                        if at == 38:
                            ffn_residual("ffn1", b + 2)
                    if has(b + 1):
                        if at == 1:
                            normalise("attention", b + 1)
                        if at == 10:
                            split_rest("q", b + 1, 0)
                        if at == 12:
                            split_rest("q", b + 1, 1)
                        if at == 13:
                            split_rest("k", b + 1, 0)
                        if at == 15:
                            split_rest("k", b + 1, 1)
                    if has(b - 1):
                        if at == 19:
                            normalise("ffn2", b - 1)
                        if at == 23:
                            token_difference("ffn2", b - 1)
                        if at == 31:
                            square_relu("ffn2", b - 1)
                        if at == 37:
                            ffn_residual("ffn2", b - 1)

            pool.wait_ge(pool_set, 4)
            for b in ITERATIONS:
                iteration(b)

        @block.scalar
        def _(act):
            act.wait_ge(consts_in, 16 * 9)
            act.activation(dcol[:, 1:2], dcol[:, 0:1], ACT.Exp, scale=-1.0).then_inc(act_set, 1)
            act.wait_ge(dve_set, 3)
            act.activation(dcol[:, 4:5], dcol[:, 3:4], ACT.Ln).then_inc(act_set, 1)
            act.wait_ge(act_set, 2)
            act.activation(w_table[:], w_table[:], ACT.Exp, scale=dcol[:, 4:5]).then_inc(act_set, 1)

            def copy_turned(k, b):
                reach(act, turned[k], b)
                if k != "attention":
                    reach(act, mixed["ffn1" if k == "retention" else k], b - 1, 2, 2)
                act.activation(xnt[k][:, 1:1 + T], BANK[k][:], ACT.Copy).then_inc(xt_ready[k], 1)

            def copy_k(b):
                reach(act, a_k, b)
                reach(act, kw_ready, b - 1)
                act.activation(k_sb[:], a_bank[:], ACT.Copy).then_inc(k_copied, 1)

            def tanh_r(b):
                reach(act, a_r, b)
                reach(act, scan_steps, b - 1, 3, 3)
                act.activation(r_tanh[:], a_bank[:], ACT.Tanh, scale=0.5).then_inc(a_tanh, 1)

            def ffn_tanh(k, b):
                reach(act, f_r[k], b)
                reach(act, gated_ready[k], b - 1)
                act.activation(f_tanh[k][:], BANK[k][:], ACT.Tanh, scale=0.5).then_inc(f_tanh_ready[k], 1)

            def ffn_relu(k, b):
                reach(act, f_k[k], b)
                reach(act, act_ready[k], b - 1)
                act.activation(k_relu[k][:], BANK[k][:], ACT.Relu).then_inc(relu_ready[k], 1)

            def project_q(b):
                reach(act, b_q, b)
                reach(act, rest["q"], b - 1, 1, 2)
                if b == 0:
                    act.wait_ge(dve_set, DVE_ALL)
                act.activation(qf["q"][:], b_bank[:], ACT.Identity, bias=bq_s[:], scale=float(SCALE))\
                    .then_inc(qf_ready["q"], 1)

            def project_k(b):
                reach(act, b_k, b)
                reach(act, rest["k"], b - 1, 1, 2)
                act.activation(qf["k"][:], b_bank[:], ACT.Identity, bias=bcol[:, 1:2])\
                    .then_inc(qf_ready["k"], 1)

            def exponentials(s, b, g, i):
                j, heads = P2_UNITS[i]
                reach(act, s2_full, b, N2 * g + i + 1, NG * N2)
                if i == 0:
                    reach(act, pv_done, b, NT * (g - 1), NG * NT)
                n = WIDTH[j] * len(heads)
                a = PT_AT[j] + WIDTH[j] * heads[0]
                act.activation(pt[s % 2][:, a:a + n], s2_bank[(g + i) % 2][:, 0:n], ACT.Exp).then_inc(exp_done, 1)

            def copy_o(s, b, g):
                reach(act, pv_done, b, NT * (g + 1), NG * NT)
                reach(act, o_turned, b, g, NG)
                act.activation(o_sb[s % 2][:], o_bank[:], ACT.Copy).then_inc(o_copied, 1)

            def copy_o_t(b):
                reach(act, c_turned, b)
                act.activation(o_t[:], c_bank[:], ACT.Copy).then_inc(ot_ready, 1)

            def iteration(b):
                for at, s, g, k in slots(b):
                    if k >= LAG and live(s):
                        exponentials(s, b, g, k - LAG)
                    if k < LAG and live(s - 1):
                        bb, gg = (b, g - 1) if g else (b - 1, NG - 1)
                        exponentials(s - 1, bb, gg, STEPS - LAG + k)
                    if k == 8 and live(s - 1):
                        bb, gg = (b, g - 1) if g else (b - 1, NG - 1)
                        copy_o(s - 1, bb, gg)
                    if has(b + 2):
                        if at == 4:
                            copy_turned("retention", b + 2)
                        if at == 6:
                            copy_k(b + 2)
                        if at == 8:
                            tanh_r(b + 2)
                        if at == 24:
                            copy_turned("ffn1", b + 2)
                        if at == 29:
                            ffn_tanh("ffn1", b + 2)
                        if at == 31:
                            ffn_relu("ffn1", b + 2)
                    if has(b + 1):
                        if at == 3:
                            copy_turned("attention", b + 1)
                        if at == 5:
                            project_q(b + 1)
                        if at == 7:
                            project_k(b + 1)
                    if has(b - 1):
                        if at == 13:
                            copy_o_t(b - 1)
                        if at == 21:
                            copy_turned("ffn2", b - 1)
                        if at == 27:
                            ffn_tanh("ffn2", b - 1)
                        if at == 29:
                            ffn_relu("ffn2", b - 1)

            act.wait_ge(pool_set, 3)
            for b in ITERATIONS:
                iteration(b)

        @block.vector
        def _(dve):
            dve.memset(k_aug[0][0:MROW], 0.0)
            dve.memset(k_aug[1][0:MROW], 0.0)
            dve.memset(k_aug[0][MROW:P], 1.0).then_inc(zeroed, 1)
            dve.memset(k_aug[1][MROW:P], 1.0).then_inc(zeroed, 1)
            dve.wait_ge(act_set, 1)
            dve.tensor_scalar(dcol[:, 2:3], dcol[:, 1:2], 1.0, None, ALU.add).then_inc(dve_set, 1)
            dve.wait_ge(dve_set, 1)
            dve.reciprocal(dcol[:, 5:6], dcol[:, 2:3]).then_inc(dve_set, 1)
            dve.wait_ge(dve_set, 2)
            dve.tensor_scalar(dcol[:, 3:4], dcol[:, 5:6], 1e-7, None, ALU.max).then_inc(dve_set, 1)
            dve.wait_ge(weights_in, 16 * 3)
            dve.tensor_reduce(bsum[:], bw, AX.X, ALU.add, apply_absolute_value=True).then_inc(bw_set, 1)
            dve.wait_ge(bw_set, 1)
            dve.tensor_scalar(bscale[:], bsum[:], 1.0 / D, 1e-5, ALU.mult, ALU.max).then_inc(bw_set, 1)
            dve.wait_ge(bw_set, 2)
            dve.tensor_scalar(bhalf[:, 0, :], bscale[:], 0.5, None, ALU.mult)
            dve.tensor_scalar(bhalf[:, 1, :], bscale[:], -0.5, None, ALU.mult).then_inc(bw_set, 1)
            dve.wait_ge(bw_set, 3)
            for i in range(4):
                dve.tensor_scalar(bw_gt, bw[:, i, :], bhalf[:, 0, i:i + 1], bscale[:, i:i + 1], ALU.is_gt, ALU.mult)
                dve.tensor_scalar(bw_lt, bw[:, i, :], bhalf[:, 1, i:i + 1], bscale[:, i:i + 1], ALU.is_lt, ALU.mult)\
                    .then_inc(bw_set, 1)
                dve.wait_ge(bw_set, 4 + 4 * i)
                dve.tensor_tensor(bw_q[:, i, :], bw_gt, bw_lt, ALU.subtract).then_inc(bw_set, 1)
                dve.wait_ge(bw_set, 5 + 4 * i)
                dve.tensor_tensor(bw_gt, bw_q[:, i, :], bw[:, i, :], ALU.subtract).then_inc(bw_set, 1)
                dve.wait_ge(bw_set, 6 + 4 * i)
                dve.tensor_tensor(bw_q[:, i, :], bw[:, i, :], bw_gt, ALU.add).then_inc(bw_set, 1)
                dve.wait_ge(bw_set, 7 + 4 * i)
            dve.tensor_scalar(wf[:, 2, :], wf[:, 2, :], 0.5, None, ALU.mult).then_inc(dve_set, 1)
            dve.wait_ge(act_set, 3)
            dve.tensor_scalar(w_table[:], w_table[:], 1.0 / CLIP_SCALE, 1.0, ALU.mult, ALU.min).then_inc(dve_set, 1)
            dve.wait_ge(pe_set, 1)
            dve.wait_ge(consts_in, 16 * 9)
            dve.tensor_copy(wa[:, 0:3, :], a_bank[:, 0:3 * P].rearrange("p (w d) -> p w d", w=3)).then_inc(dve_set, 1)
            dve.tensor_scalar(wa[:, 3, :], a_bank[:, 3 * P:4 * P], lnw[:, 0:1], None, ALU.mult).then_inc(dve_set, 1)
            dve.wait_ge(pool_set, 4)
            dve.tensor_scalar(bv_b[:], ones_f[:], bcol[:, 2:3], None, ALU.mult).then_inc(dve_set, 1)
            dve.tensor_scalar(bq_s[:], bcol[:, 0:1], float(SCALE), None, ALU.mult).then_inc(dve_set, 1)
            dve.wait_ge(pe_set, 2)
            dve.tensor_tensor(bias_o[:], c_bank[:, 0:D], bo_b[:], ALU.add).then_inc(dve_set, 1)

            def statistics(k, b):
                p = b % 2
                wait_source(dve, k, b, p)
                for t in range(NT):
                    last = dve.bn_stats(st[k][:, t, :], SRC[k][p][:, t, :])
                last.then_inc(stats[k], 1)
                reach(dve, stats[k], b, 1, 2)
                reach(dve, norm[k], b - 1, 3, 4)
                for t in range(NT):
                    last = dve.bn_aggr(mv[k][:, t, :], st[k][:, t, :])
                last.then_inc(stats[k], 1)

            def scan_state(b):
                reach(dve, a_v, b)
                reach(dve, kw_ready, b)
                dve.tensor_tensor(kvw[:], a_bank[:], kw[:], ALU.mult).then_inc(scan_steps, 1)
                reach(dve, scan_steps, b, 1, 3)
                dve.tensor_tensor_scan(state[:], dcol[:, 3:4].to_broadcast([P, T]), kvw[:], 0.0, ALU.mult, ALU.add)\
                    .then_inc(scan_steps, 1)

            def gate_state(b):
                reach(dve, a_tanh, b)
                reach(dve, scan_steps, b, 2, 3)
                reach(dve, a_y, b - 1)
                dve.scalar_tensor_tensor(out=u[:], in0=r_tanh[:], scalar=1.0, in1=state[:],
                                         op0=ALU.add, op1=ALU.mult).then_inc(scan_steps, 1)

            def mean_square(b):
                reach(dve, a_ss, b)
                reach(dve, rrms_ready, b - 1)
                dve.tensor_scalar(msq[:], a_bank[:, 0:NT], 1.0 / D, 4.0 * RMS_EPS, ALU.mult, ALU.add)\
                    .then_inc(msq_ready, 1)

            def retention_residual(b):
                p = b % 2
                reach(dve, a_y, b)
                reach(dve, rrms_ready, b)
                for t in range(NT):
                    last = dve.scalar_tensor_tensor(out=x_1[p][:, t, :], in0=a_bank[:, t * P:(t + 1) * P],
                                                    scalar=rrms[:, t:t + 1], in1=x_in[p][:, t, :],
                                                    op0=ALU.mult, op1=ALU.add)
                last.then_inc(x1_ready, 1)

            def mix(k, b):
                reach(dve, dx_ready[k], b)
                reach(dve, f_k[k], b - 1)
                if k == "ffn2":
                    reach(dve, c_y, b)
                for i, dst in enumerate((xr[k], xk[k])):
                    dve.scalar_tensor_tensor(out=dst[:], in0=dx[k][:], scalar=mu_sb[:, i:i + 1],
                                             in1=xnt[k][:, 0:T], op0=ALU.mult, op1=ALU.add).then_inc(mixed[k], 1)

            def gate_ffn(k, b):
                reach(dve, f_v[k], b)
                reach(dve, f_tanh_ready[k], b)
                reach(dve, ffn_out[k], b - 1)
                dve.scalar_tensor_tensor(out=gated[k][:], in0=f_tanh[k][:], scalar=1.0, in1=BANK[k][:],
                                         op0=ALU.add, op1=ALU.mult).then_inc(gated_ready[k], 1)

            def cast_part(n, b, i):
                if i == 0:
                    reach(dve, qf_ready[n], b)
                    if b:
                        dve.wait_ge(parts_out[(b - 1) % 2], 96 * ((b - 1) // 2 + 1))
                    dve.tensor_copy(parts[n][:, 0, :], qf[n][:]).then_inc(cast[n], 1)
                else:
                    reach(dve, rest[n], b, 1, 2)
                    dve.tensor_copy(parts[n][:, 1, :], qres[n][:]).then_inc(cast[n], 1)

            def copy_v(b):
                p = b % 2
                reach(dve, b_v, b)
                reach(dve, pv_done, b - 2, NG * NT, NG * NT)
                if b < 2:
                    dve.wait_ge(pool_set, 6)
                dve.tensor_copy(v_aug[p][:, :, :, 0:HD], b_bank[:].rearrange("p (t h d) -> p t h d", t=NT, h=H))\
                    .then_inc(v_ready, 1)

            def block_maxima(b, g, i):
                nxt = (g + 1) % 2
                unit = P1_UNITS[i]
                h, q = unit[0]
                bank = s1_bank[(g + 1 + i) % 2]
                reach(dve, s1_full, b, N1 * g + 10 + 2 + i, NG * N1)
                if i == 0:
                    reach(dve, mparts_ready, b, 2 * g, 2 * NG)
                if q == 3:
                    dve.tensor_reduce(negm[nxt][:, h, 3:4], bank[:], AX.X, ALU.max, negate=True).then_inc(s1_free, 1)
                elif q == 1:
                    dve.tensor_reduce(negm[nxt][:, h:h + 2, 1:2].rearrange("p h o -> p (h o)"),
                                      bank[:].rearrange("p (h k) -> p h k", h=2),
                                      AX.X, ALU.max, negate=True).then_inc(s1_free, 1)
                else:
                    dve.tensor_reduce(bmax[nxt][:, h, :], bank[:].rearrange("p (j k) -> p j k", j=NT),
                                      AX.X, ALU.max).then_inc(s1_free, 1)

            def group_maxima(b, g):
                nxt = (g + 1) % 2
                reach(dve, s1_free, b, N1 * g + 10 + N1, NG * N1)
                dve.tensor_reduce(negm[nxt][:, :, 2:3].rearrange("p h o -> p (h o)"), bmax[nxt][:, :, 0:3],
                                  AX.X, ALU.max, negate=True).then_inc(negm_ready, 1)
                dve.tensor_scalar(negm[nxt][:, :, 0], bmax[nxt][:, :, 3], -1.0, None, ALU.mult)\
                    .then_inc(negm_ready, 1)

            def copy_max_rows(s, b, g):
                p = s % 2
                reach(dve, s1_full, b, N1 * g + 10 + 1, NG * N1)
                if s >= 2:
                    dve.wait_ge(m_loaded[p], 32 * (s // 2))
                dve.tensor_copy(m_rows[p][:], s1_bank[g % 2][0:2 * G * NT, 0:P // 2].bitcast(BF16))\
                    .then_inc(s1_free, 1)

            def normalise_o(s, b, g):
                reach(dve, o_turned, b, g + 1, NG)
                o = o_bank[:].rearrange("p (t h c) -> p t h c", t=NT, h=G)
                dve.reciprocal(rsum[:], o[:, :, :, HD]).then_inc(o_normed, 1)
                reach(dve, o_normed, b, 2 * g + 1, 2 * NG)
                if g == 0:
                    reach(dve, c_turned, b - 1)
                dst = o_tm[(s // NG) % 2][:, :, G * HD * g:G * HD * (g + 1)].rearrange("p t (h d) -> p t h d", h=G)
                dve.tensor_tensor(dst, o[:, :, :, 0:HD],
                                  rsum[:].rearrange("p t (h o) -> p t h o", o=1).to_broadcast([P, NT, G, HD]),
                                  ALU.mult).then_inc(o_normed, 1)

            def attention_residual(b):
                p = b % 2
                reach(dve, c_y, b)
                reach(dve, x2b_ready, b)
                dve.tensor_tensor(x_3[p][:].rearrange("p t d -> p (t d)"), c_bank[:],
                                  x_2b[:].rearrange("p t d -> p (t d)"), ALU.add).then_inc(x3_ready, 1)

            def iteration(b):
                for at, s, g, k in slots(b):
                    if k == 0 and live(s):
                        copy_max_rows(s, b, g)
                    if k == 0 and live(s - 2):
                        bb, gg = (b, g - 2) if g >= 2 else (b - 1, g - 2 + NG)
                        normalise_o(s - 2, bb, gg)
                    if k >= 1 and live(s + 1):
                        block_maxima(b, g, k - 1)
                        if k == STEPS - 1:
                            group_maxima(b, g)
                    if has(b + 2):
                        if at == 1:
                            statistics("retention", b + 2)
                        if at == 11:
                            scan_state(b + 2)
                        if at == 12:
                            gate_state(b + 2)
                        if at == 17:
                            mean_square(b + 2)
                        if at == 20:
                            retention_residual(b + 2)
                            statistics("ffn1", b + 2)
                        if at == 27:
                            mix("ffn1", b + 2)
                        if at == 36:
                            gate_ffn("ffn1", b + 2)
                    if has(b + 1):
                        if at == 0:
                            statistics("attention", b + 1)
                        if at == 8:
                            cast_part("q", b + 1, 0)
                        if at == 9:
                            copy_v(b + 1)
                        if at == 10:
                            cast_part("k", b + 1, 0)
                        if at == 11:
                            cast_part("q", b + 1, 1)
                        if at == 14:
                            cast_part("k", b + 1, 1)
                    if has(b - 1):
                        if at == 17:
                            attention_residual(b - 1)
                            statistics("ffn2", b - 1)
                        if at == 25:
                            mix("ffn2", b - 1)
                        if at == 34:
                            gate_ffn("ffn2", b - 1)

            for b in ITERATIONS:
                iteration(b)

        @block.tensor
        def _(pe):
            pe.wait_ge(consts_in, 16 * 9)
            for i in range(4):
                pe.wait_ge(bw_set, 7 + 4 * i)
                last = pe.transpose(a_bank[:, i * P:(i + 1) * P], bw_q[:, i, :], id_f[:])
            last.then_inc(pe_set, 1)
            pe.wait_ge(dve_set, 9)
            pe.matmul(c_bank[:, 0:D], bv_b[:], wb[:, 3, :], start=True, stop=True).then_inc(pe_set, 1)
            pe.wait_ge(dve_set, DVE_ALL)

            def turn(k, b):
                reach(pe, norm[k], b, 4, 4)
                if k == "retention":
                    reach(pe, gated_ready["ffn1"], b - 1)
                elif k == "ffn1":
                    reach(pe, x1_ready, b)
                elif k == "attention":
                    reach(pe, v_ready, b - 1)
                else:
                    reach(pe, x3_ready, b)
                for t in range(NT):
                    last = pe.transpose(BANK[k][:, t * P:(t + 1) * P], xn[k][:, t, :], id_f[:])
                last.then_inc(turned[k], 1)

            def to_channels(bank, weight, src, signal):
                pe.matmul(bank[:], weight, src, start=True, stop=True).then_inc(signal, 1)

            def to_tokens(bank, src, weight, signal):
                for t in range(NT):
                    last = pe.matmul(bank[:, t * P:(t + 1) * P], src[:, t * P:(t + 1) * P], weight,
                                     start=True, stop=True)
                last.then_inc(signal, 1)

            def retention_k(b):
                reach(pe, xt_ready["retention"], b)
                to_channels(a_bank, wa[:, 1, :], xnt["retention"][:, 1:1 + T], a_k)

            def retention_r(b):
                reach(pe, k_copied, b)
                to_channels(a_bank, wa[:, 0, :], xnt["retention"][:, 1:1 + T], a_r)

            def retention_v(b):
                reach(pe, a_tanh, b)
                to_channels(a_bank, wa[:, 2, :], xnt["retention"][:, 1:1 + T], a_v)

            def sum_squares(b):
                reach(pe, usq_ready, b)
                reach(pe, scan_steps, b, 1, 3)
                for t in range(NT):
                    last = pe.matmul(a_bank[:, t:t + 1], usq[:, t * P:(t + 1) * P], ones_f[:, 0:1],
                                     start=True, stop=True)
                last.then_inc(a_ss, 1)

            def retention_out(b):
                reach(pe, msq_ready, b)
                reach(pe, scan_steps, b, 3, 3)
                to_tokens(a_bank, u, wa[:, 3, :], a_y)

            def ffn_r(k, b):
                reach(pe, mixed[k], b, 1, 2)
                to_tokens(BANK[k], xr[k], wf[:, 0, :], f_r[k])

            def ffn_k(k, b):
                reach(pe, mixed[k], b, 2, 2)
                reach(pe, f_tanh_ready[k], b)
                to_channels(BANK[k], wf[:, 1, :], xk[k][:], f_k[k])

            def ffn_v(k, b):
                reach(pe, act_ready[k], b)
                to_tokens(BANK[k], k_act[k], wf[:, 2, :], f_v[k])

            def attention_q(b):
                reach(pe, xt_ready["attention"], b)
                to_channels(b_bank, wb[:, 0, :], xnt["attention"][:, 1:1 + T], b_q)

            def attention_k(b):
                reach(pe, qf_ready["q"], b)
                to_channels(b_bank, wb[:, 1, :], xnt["attention"][:, 1:1 + T], b_k)

            def attention_v(b):
                reach(pe, qf_ready["k"], b)
                to_tokens(b_bank, xnt["attention"][:, 1:1 + T], wb[:, 2, :], b_v)

            def first_pass(b, g, i):
                nb, ng = (b, g + 1) if g + 1 < NG else (b + 1, 0)
                p = nb % 2
                if ng == 0 and i == 0:
                    pe.wait_ge(aug_loaded[p], 16 * 9 * (nb // 2 + 1))
                    if nb < 2:
                        pe.wait_ge(aug_in, 16 * 4)
                bank = s1_bank[(g + 1 + i) % 2]
                reach(pe, s1_free, b, N1 * g + 10 + 1 + i - 1, NG * N1)
                col = 0
                for h, q in P1_UNITS[i]:
                    n = P * (q + 1)
                    head = G * ng + h
                    pe.matmul(bank[:, col:col + n], q_aug[p][0:MROW, head, q * P:(q + 1) * P],
                              k_aug[p][0:MROW, head, 0:n], start=True, stop=False)
                    last = pe.matmul(bank[:, col + n - P:col + n], id_b[:], mask_b[:], start=False, stop=True)
                    col += n
                last.then_inc(s1_full, 1)

            def turn_maxima(s, b, g):
                reach(pe, mparts_ready, b, 2 * g + 2, 2 * NG)
                reach(pe, s1_free, b, N1 * g + 10 - 1, NG * N1)
                pe.transpose(s1_bank[g % 2][0:2 * G * NT, 0:P // 2].bitcast(BF16),
                             m_parts[s % 2][:].rearrange("p a m -> p (a m)"), id_b[:]).then_inc(s1_full, 1)

            def second_pass(s, b, g, i):
                j, heads = P2_UNITS[i]
                p = (s // NG) % 2
                if i == 0:
                    pe.wait_ge(m_loaded[s % 2], 32 * (s // 2 + 1))
                reach(pe, exp_done, b, N2 * g + i - 1, NG * N2)
                w = WIDTH[j]
                for c, h in enumerate(heads):
                    last = pe.matmul(s2_bank[(g + i) % 2][:, c * w:(c + 1) * w],
                                     k_aug[p][0:KROWS, G * g + h, j * P:(j + 1) * P],
                                     q_aug[p][0:KROWS, G * g + h, j * P:T], start=True, stop=True)
                last.then_inc(s2_full, 1)

            def weigh_values(s, b, g, j):
                p = (s // NG) % 2
                reach(pe, masked, b, NT * g + j + 1, NG * NT)
                if j == 0:
                    reach(pe, o_normed, b, 2 * g, 2 * NG)
                    if g == 0:
                        reach(pe, v_ready, b)
                w = WIDTH[j]
                for h in range(G):
                    a = PT_AT[j] + w * h
                    last = pe.matmul(o_bank[VW * h:VW * (h + 1), j * P:T], v_aug[p][:, j, G * g + h, :],
                                     pt[s % 2][:, a:a + w], start=(j == 0), stop=(j == NT - 1))
                last.then_inc(pv_done, 1)

            def turn_o(s, b, g):
                reach(pe, o_copied, b, g + 1, NG)
                for t in range(NT):
                    last = pe.transpose(o_bank[:, t * P:(t + 1) * P], o_sb[s % 2][:, t * P:(t + 1) * P], id_f[:])
                last.then_inc(o_turned, 1)

            def turn_heads(b):
                reach(pe, o_normed, b, 2 * NG, 2 * NG)
                reach(pe, gated_ready["ffn2"], b - 1)
                for t in range(NT):
                    last = pe.transpose(c_bank[:, t * P:(t + 1) * P], o_tm[b % 2][:, t, :], id_f[:])
                last.then_inc(c_turned, 1)

            def attention_out(b):
                reach(pe, ot_ready, b)
                to_tokens(c_bank, o_t, wb[:, 3, :], c_y)

            def iteration(b):
                for at, s, g, k in slots(b):
                    before = (b, g - 1) if g else (b - 1, NG - 1)
                    if k == 0 and live(s):
                        turn_maxima(s, b, g)
                    if k >= 1 and live(s + 1):
                        first_pass(b, g, k - 1)
                    if k >= LAG and live(s):
                        second_pass(s, b, g, k - LAG)
                    if k < LAG and live(s - 1):
                        second_pass(s - 1, *before, STEPS - LAG + k)
                    if k in PV_STEP and live(s - 1):
                        weigh_values(s - 1, *before, PV_STEP[k])
                    if k == 9 and live(s - 1):
                        turn_o(s - 1, *before)
                    if has(b + 2):
                        if at == 3:
                            turn("retention", b + 2)
                        if at == 5:
                            retention_k(b + 2)
                        if at == 7:
                            retention_r(b + 2)
                        if at == 9:
                            retention_v(b + 2)
                        if at == 16:
                            sum_squares(b + 2)
                        if at == 18:
                            retention_out(b + 2)
                        if at == 23:
                            turn("ffn1", b + 2)
                        if at == 28:
                            ffn_r("ffn1", b + 2)
                        if at == 30:
                            ffn_k("ffn1", b + 2)
                        if at == 34:
                            ffn_v("ffn1", b + 2)
                    if has(b + 1):
                        if at == 2:
                            turn("attention", b + 1)
                        if at == 4:
                            attention_q(b + 1)
                        if at == 6:
                            attention_k(b + 1)
                        if at == 8:
                            attention_v(b + 1)
                    if has(b - 1):
                        if at == 12:
                            turn_heads(b - 1)
                        if at == 14:
                            attention_out(b - 1)
                        if at == 20:
                            turn("ffn2", b - 1)
                        if at == 26:
                            ffn_r("ffn2", b - 1)
                        if at == 28:
                            ffn_k("ffn2", b - 1)
                        if at == 33:
                            ffn_v("ffn2", b - 1)

            for b in ITERATIONS:
                iteration(b)


def bf16_parts(a, n):
    out = []
    for _ in range(n):
        part = a.astype(mybir.dt.np(BF16))
        out.append(part)
        a = (a - part.astype(np.float32)).astype(np.float32)
    return out


def constants():
    bf = mybir.dt.np(BF16)
    slope = np.power(np.float32(2.0), (-8.0 * np.arange(1, H + 1) / H).astype(np.float32)).astype(np.float32)
    token = np.arange(T)
    lo, hi = (token % 256).astype(bf), (token - token % 256).astype(bf)
    aug_q = np.zeros((NCONST, H, T), bf)
    aug_k = np.zeros((NCONST, H, T), bf)
    for i, s in enumerate(bf16_parts(slope, 3)):
        aug_q[4 * i] = aug_q[4 * i + 1] = s[:, None]
        aug_k[4 * i], aug_k[4 * i + 1] = lo, hi
        aug_q[4 * i + 2], aug_q[4 * i + 3] = lo, hi
        aug_k[4 * i + 2] = aug_k[4 * i + 3] = -s[:, None]
    for r in range(1, T // SUB):
        aug_k[NBIAS + r - 1] = (token // SUB == r).astype(bf)
        aug_q[NBIAS + r - 1] = np.where(token // SUB < r, np.float32(FAR), np.float32(0)).astype(bf)
    causal = np.where(np.arange(P)[None, :] > np.arange(P)[:, None], np.float32(FAR), np.float32(0)).astype(bf)
    return {
        "ident": np.eye(P, dtype=np.float32), "ident_b": np.eye(P, dtype=np.float32).astype(bf), "causal": causal,
        "pos": np.broadcast_to(np.arange(T, dtype=np.float32), (P, T)).copy(), "aug_q": aug_q, "aug_k": aug_k,
    }


def kernel(**inputs):
    import concourse.bacc as _bacc
    from concourse.bass_utils import run_bass_kernel_spmd as _run

    a = {k: np.asarray(v) for k, v in inputs.items()}

    def col(*names):
        return np.ascontiguousarray(np.stack([a[n] for n in names], axis=1))

    arrays = {
        "x": np.ascontiguousarray(a["L0_attn_a_x"]),
        "w_a": np.ascontiguousarray(np.stack([a[f"L0_attn_a_W{n}"] for n in "rkvo"], axis=1)),
        "w_f": np.ascontiguousarray(np.stack([a[f"L0_ffn_W_{n}"].T for n in "rkv"], axis=1)),
        "w_b": np.ascontiguousarray(np.stack([a[f"L0_attn_b_W{n}"].T for n in "qkvo"], axis=1)),
        "decay": col("L0_attn_a_decay"), "ln_w": col("L0_attn_a_ln_w"),
        "mu": col("L0_ffn_mu_r", "L0_ffn_mu_k"),
        "b_cols": col("L0_attn_b_bq", "L0_attn_b_bk", "L0_attn_b_bv"),
        "bo_row": np.ascontiguousarray(a["L0_attn_b_bo"].reshape(1, D)),
        **constants(),
    }
    nc = _bacc.Bacc("TRN2", target_bir_lowering=False, num_devices=1)
    args = {k: nc.dram_tensor(k, v.shape, mybir.dt.from_np(v.dtype), kind="ExternalInput").ap()
            for k, v in arrays.items()}
    args["out"] = nc.dram_tensor("out", (B, T, D), F32, kind="ExternalOutput").ap()
    build(nc, **args)
    r = _run(nc, [arrays], core_ids=[0])
    return r.results[0]["out"]
```

```python
from contextlib import ExitStack

import numpy as np

import concourse.bass as bass
from concourse import mybir

F32 = mybir.dt.float32
BF16 = mybir.dt.bfloat16
ACT = mybir.ActivationFunctionType
ALU = mybir.AluOpType
AX = mybir.AxisListType

P = 128
B = 8
T = 512
NT = T // P
D = 128
H = 16
HD = D // H
G = 4
NG = H // G
VW = 32
SCALE = 1.0 / np.sqrt(HD)
LN_EPS = 1e-5
RMS_EPS = 1e-6
CLIP_SCALE = 1e-10

SUB = 16
NBIAS = 12
NCONST = NBIAS + T // SUB - 1
FAR = -1e30
NSPLIT = 6 * HD
MROW = 96
KROWS = MROW + 2

WIDTH = [T - P * j for j in range(NT)]
PT_AT = [G * sum(WIDTH[:j]) for j in range(NT)]
PT_COLS = G * sum(WIDTH)

P1_UNITS = [[(h, 3)] for h in range(G)] + [[(0, 1), (1, 1)], [(2, 1), (3, 1)]] + [[(h, 2), (h, 0)] for h in range(G)]
P2_UNITS = [(0, [h]) for h in range(G)] + [(1, [h]) for h in range(G)] + [(2, [0, 1]), (2, [2, 3]), (3, [0, 1, 2, 3])]
N1, N2 = len(P1_UNITS) + 1, len(P2_UNITS)
STEPS = 11
EXPS_OF = [sum(1 for j, _ in P2_UNITS if j <= jj) for jj in range(NT)]
TURN_AT = 3

SLOT_STEP = {
    "second pass": 7,
    "mask 0": 11,
    "mask 1": 15,
    "mask 2": 17,
    "mask 3": 17,
    "weigh values 0": 14,
    "weigh values 1": 16,
    "weigh values 2": 18,
    "weigh values 3": 20,
    "copy o": 21,
    "turn o": 23,
    "normalise o": 24,
}

SP_STEP = {
    "parts q": 23,
    "parts k": 23,
    "load": 23,
    "store": 40,
}
DELAY_STEP = {
    "retention 0": -31,
    "retention 1": -2,
    "retention 2": 0,
    "ffn1 0": -24,
    "ffn1 1": 0,
    "ffn1 2": 0,
    "attention 0": 3,
    "attention 1": 0,
    "attention 2": 0,
    "ffn2 5": 0,
    "ffn2 6": 0,
    "ffn2 7": 34,
}
POOL_STEP = {
    "residual bias": 22,
    "normalise retention": 2,
    "key times table": 9,
    "square u": 15,
    "rms power": 18,
    "normalise ffn1": 20,
    "token difference ffn1": 27,
    "square relu ffn1": 30,
    "ffn residual ffn1": 37,
    "normalise attention": 0,
    "split rest q 0": 6,
    "split rest q 1": 13,
    "split rest k 0": 13,
    "split rest k 1": 16,
    "normalise ffn2": 19,
    "token difference ffn2": 22,
    "square relu ffn2": 29,
    "ffn residual ffn2": 33,
}
ACT_STEP = {
    "copy turned retention": 5,
    "copy k": 8,
    "tanh r": 10,
    "copy turned ffn1": 23,
    "ffn tanh ffn1": 30,
    "ffn relu ffn1": 31,
    "copy turned attention": 3,
    "project q": 4,
    "project k": 6,
    "copy o t": 12,
    "copy turned ffn2": 22,
    "ffn tanh ffn2": 27,
    "ffn relu ffn2": 29,
}
DVE_STEP = {
    "statistics retention": 1,
    "scan state": 13,
    "gate state": 15,
    "mean square": 18,
    "retention residual": 18,
    "mix ffn1": 28,
    "gate ffn ffn1": 36,
    "statistics attention": 0,
    "cast part q 0": 8,
    "copy v": 9,
    "cast part k 0": 10,
    "cast part q 1": 11,
    "cast part k 1": 13,
    "attention residual": 15,
    "mix ffn2": 26,
    "gate ffn ffn2": 33,
}
PE_STEP = {
    "turn retention": 6,
    "retention k": 7,
    "retention r": 11,
    "retention v": 12,
    "sum squares": 17,
    "retention out": 19,
    "turn ffn1": 24,
    "ffn r ffn1": 29,
    "ffn k ffn1": 32,
    "ffn v ffn1": 35,
    "turn attention": 3,
    "attention q": 4,
    "attention k": 6,
    "attention v": 8,
    "turn heads": 13,
    "attention out": 15,
    "turn ffn2": 22,
    "ffn r ffn2": 27,
    "ffn k ffn2": 29,
    "ffn v ffn2": 33,
}


def build(nc, x, w_a, w_f, w_b, decay, ln_w, mu, b_cols, bo_row, ident, ident_b, causal, pos, aug_q, aug_k, out):
    ctx = ExitStack()
    with ctx:
        def sb(name, shape, dt=F32):
            return ctx.enter_context(nc.sbuf_tensor(name, shape, dt))

        def ps(name):
            return ctx.enter_context(nc.psum_tensor(name, [P, T], F32))

        def sem(name):
            return ctx.enter_context(nc.semaphore(name))

        s1_bank = [ps("s1_bank0"), ps("s1_bank1")]
        s2_bank = [ps("s2_bank0"), ps("s2_bank1")]
        o_bank = ps("o_bank")
        a_bank = ps("a_bank")
        b_bank = ps("b_bank")
        c_bank = ps("c_bank")

        id_f = sb("id_f", [P, P])
        id_b = sb("id_b", [P, P], BF16)
        mask_b = sb("mask_b", [P, P], BF16)
        w_table = sb("w_table", [P, T])
        bsum = sb("bsum", [P, 4])
        bscale = sb("bscale", [P, 4])
        bhalf = sb("bhalf", [P, 2, 4])
        wa = sb("wa", [P, 4, P])
        wf = sb("wf", [P, 3, P])
        wb = sb("wb", [P, 4, P])
        dcol = sb("dcol", [P, 6])
        lnw = sb("lnw", [P, 1])
        mu_sb = sb("mu_sb", [P, 2])
        bcol = sb("bcol", [P, 3])
        bq_s = sb("bq_s", [P, 1])
        ones_f = sb("ones_f", [P, P])
        bv_b = sb("bv_b", [P, P])
        bo_b = sb("bo_b", [P, P])
        bias_o = sb("bias_o", [P, P])
        neg_half = sb("neg_half", [P, NT])

        x_in = [sb(f"x_in{p}", [P, NT, D]) for p in range(2)]
        x_1 = [sb("x_1", [P, NT, D])] * 2
        x_2 = [sb(f"x_2{p}", [P, NT, D]) for p in range(2)]
        x_2b = sb("x_2b", [P, NT, D])
        x_3 = [sb("x_3", [P, NT, D])] * 2
        LN = ["retention", "ffn1", "attention", "ffn2"]
        st = {k: sb(f"st_{k}", [P, NT, 6]) for k in LN}
        mv = {k: sb(f"mv_{k}", [P, NT, 2]) for k in LN}
        ve = {k: sb(f"ve_{k}", [P, NT]) for k in LN}
        rstd = {k: sb(f"rstd_{k}", [P, NT]) for k in LN}
        nmean = {k: sb(f"nmean_{k}", [P, NT]) for k in LN}
        xn = {k: sb(f"xn_{k}", [P, NT, D]) for k in LN if k != "attention"}
        xn["attention"] = xn["ffn1"]
        xnt = {k: sb(f"xnt_{k}", [P, 1 + T]) for k in LN}

        k_sb = sb("k_sb", [P, T])
        kw = sb("kw", [P, T])
        kvw = sb("kvw", [P, T])
        state = k_sb
        r_tanh = sb("r_tanh", [P, T])
        u = kvw
        usq = kw
        msq = sb("msq", [P, NT])
        rrms = sb("rrms", [P, NT])

        FF = ["ffn1", "ffn2"]
        dx = {k: sb(f"dx_{k}", [P, T]) for k in FF}
        xr = {k: sb(f"xr_{k}", [P, T]) for k in FF}
        xk = {k: sb(f"xk_{k}", [P, T]) for k in FF}
        f_tanh = {k: sb(f"f_tanh_{k}", [P, T]) for k in FF}
        k_relu = {k: sb(f"k_relu_{k}", [P, T]) for k in FF}
        k_act = k_relu
        gated = dx
        x_out = dx["ffn2"][:].rearrange("p (t d) -> p t d", t=NT)

        qf = {n: sb(f"{n}f", [P, T]) for n in "qk"}
        qres = {n: sb(f"{n}res", [P, T]) for n in "qk"}
        parts = {n: sb(f"{n}parts", [P, 3, T], BF16) for n in "qk"}
        q_aug = [sb(f"q_aug{p}", [P, H, T], BF16) for p in range(2)]
        k_aug = [sb(f"k_aug{p}", [P, H, T], BF16) for p in range(2)]
        v_aug = [sb(f"v_aug{p}", [P, NT, H, VW]) for p in range(2)]
        q_dram = [nc.dram_tensor(f"q_dram{p}", [H, 3, HD, T], BF16, kind="Internal").ap() for p in range(2)]
        k_dram = [nc.dram_tensor(f"k_dram{p}", [H, 3, HD, T], BF16, kind="Internal").ap() for p in range(2)]

        bmax = [sb(f"bmax{p}", [P, G, NT]) for p in range(2)]
        negm = [sb(f"negm{p}", [P, G, NT]) for p in range(2)]
        m_parts = [sb(f"m_parts{p}", [P, 2, G * NT], BF16) for p in range(2)]
        m_rows = [sb(f"m_rows{p}", [2 * G * NT, P], BF16) for p in range(2)]
        pt = [sb(f"pt{p}", [P, PT_COLS]) for p in range(2)]
        bw = pt[1][:, 0:4 * P].rearrange("p (w c) -> p w c", w=4)
        bw_q = pt[1][:, 4 * P:8 * P].rearrange("p (w c) -> p w c", w=4)
        bw_gt = pt[1][:, 8 * P:9 * P]
        bw_lt = pt[1][:, 9 * P:10 * P]
        o_sb = [sb("o_sb", [P, T])] * 2
        rsum = sb("rsum", [P, NT, G])
        o_tm = [sb("o_tm", [P, NT, D])] * 2
        o_t = xr["ffn2"]

        consts_in = sem("consts_in")
        weights_in = sem("weights_in")
        aug_in = sem("aug_in")
        pool_set = sem("pool_set")
        dve_set = sem("dve_set")
        act_set = sem("act_set")
        pe_set = sem("pe_set")
        bw_set = sem("bw_set")
        x_loaded = [sem(f"x_loaded{p}") for p in range(2)]
        stored = [sem(f"stored{p}") for p in range(2)]
        stats = {k: sem(f"stats_{k}") for k in LN}
        norm = {k: sem(f"norm_{k}") for k in LN}
        turned = {k: sem(f"turned_{k}") for k in LN}
        xt_ready = {k: sem(f"xt_{k}") for k in LN}
        a_k, a_r, a_v, a_ss, a_y = (sem(n) for n in ("a_k", "a_r", "a_v", "a_ss", "a_y"))
        k_copied, a_tanh, kw_ready, usq_ready, rrms_ready = (
            sem(n) for n in ("k_copied", "a_tanh", "kw_ready", "usq_ready", "rrms_ready"))
        scan_steps = sem("scan_steps")
        msq_ready = sem("msq_ready")
        x1_ready = sem("x1_ready")
        dx_ready = {k: sem(f"dx_{k}_ready") for k in FF}
        mixed = {k: sem(f"mixed_{k}") for k in FF}
        f_r = {k: sem(f"f_r_{k}") for k in FF}
        f_k = {k: sem(f"f_k_{k}") for k in FF}
        f_v = {k: sem(f"f_v_{k}") for k in FF}
        f_tanh_ready = {k: sem(f"f_tanh_ready_{k}") for k in FF}
        relu_ready = {k: sem(f"relu_ready_{k}") for k in FF}
        act_ready = {k: sem(f"act_ready_{k}") for k in FF}
        gated_ready = {k: sem(f"gated_ready_{k}") for k in FF}
        ffn_out = {k: sem(f"ffn_out_{k}") for k in FF}
        x2b_ready = sem("x2b_ready")
        b_q, b_k, b_v = sem("b_q"), sem("b_k"), sem("b_v")
        qf_ready = {n: sem(f"{n}f_ready") for n in "qk"}
        cast = {n: sem(f"{n}_cast") for n in "qk"}
        rest = {n: sem(f"{n}_rest") for n in "qk"}
        v_ready = sem("v_ready")
        parts_out = [sem(f"parts_out{p}") for p in range(2)]
        aug_loaded = [sem(f"aug_loaded{p}") for p in range(2)]
        s1_full, s1_free = sem("s1_full"), sem("s1_free")
        negm_ready = sem("negm_ready")
        mparts_ready = sem("mparts_ready")
        m_loaded = [sem(f"m_loaded{p}") for p in range(2)]
        s2_full, exp_done = sem("s2_full"), sem("exp_done")
        masked, pv_done = sem("masked"), sem("pv_done")
        o_copied, o_turned = sem("o_copied"), sem("o_turned")
        o_normed = sem("o_normed")
        c_turned, ot_ready, c_y, x3_ready = sem("c_turned"), sem("ot_ready"), sem("c_y"), sem("x3_ready")

        BANK = {"retention": a_bank, "ffn1": b_bank, "attention": b_bank, "ffn2": c_bank}
        SRC = {"retention": x_in, "ffn1": x_1, "attention": x_2, "ffn2": x_3}
        DST = {"ffn1": x_2, "ffn2": [x_out, x_out]}

        def reach(eng, s, b, k=1, n=1):
            v = n * b + k
            if isinstance(v, int) and v <= 0:
                return
            eng.wait_ge(s, v)

        def wait_source(eng, k, b, p):
            if k == "retention":
                eng.wait_ge(x_loaded[p], 16 * (b // 2 + 1))
            elif k == "ffn1":
                reach(eng, x1_ready, b)
            elif k == "attention":
                reach(eng, ffn_out["ffn1"], b)
            else:
                reach(eng, x3_ready, b)

        block = ctx.enter_context(nc.Block())

        ITERATIONS = range(-3, B + 2)
        LEAD = {"retention": 2, "ffn1": 2, "attention": 1, "ffn2": -1, "residual bias": 0, "load": 4}

        def s1_turn(b, g, i):
            if i is None:
                return 0 if (b, g) == (B - 1, NG - 1) else TURN_AT
            return i if i < TURN_AT and b >= 0 else i + 1

        def s1_at(b, g, i=None):
            return N1 * g + N1 - 1 + s1_turn(b, g, i)

        def s1_of(b, g, i=None):
            return s1_bank[(g + s1_turn(b, g, i)) % 2]

        def slots(b):
            for at in range(NG * STEPS):
                g, k = divmod(at, STEPS)
                yield at, NG * b + g, g, k

        def live(s):
            return 0 <= s < NG * B

        DVE_TABLE, DVE_BIAS, DVE_ALL = 5, 10, 10

        def sequence_at(stage, offset, b, at):
            for n in range(B):
                late = DELAY_STEP.get(f"{stage} {n}", 0)
                if NG * STEPS * (n - LEAD[stage]) + offset + late == NG * STEPS * b + at:
                    yield n

        def due(offset, b, g, k):
            d, step = divmod(offset, STEPS)
            if k == step and live(NG * b + g - d):
                yield NG * b + g - d, b + (g - d) // NG, (g - d) % NG

        @block.sync
        def _(sp):
            sp.dma_start(bw, w_a).then_inc(weights_in, 16)
            sp.dma_start(id_f[:], ident).then_inc(consts_in, 16)
            sp.dma_start(x_in[0][:], x[0].rearrange("(t p) d -> p t d", p=P)).then_inc(x_loaded[0], 16)
            sp.dma_start(w_table[:], pos).then_inc(consts_in, 16)
            sp.dma_start(dcol[:, 0:1], decay).then_inc(consts_in, 16)
            sp.dma_start(lnw[:], ln_w).then_inc(consts_in, 16)
            sp.dma_start(mu_sb[:], mu).then_inc(consts_in, 16)
            sp.dma_start(bcol[:], b_cols).then_inc(consts_in, 16)
            sp.dma_start(bo_b[:], bo_row.to_broadcast([P, D])).then_inc(consts_in, 16)
            sp.dma_start(wf[:], w_f).then_inc(weights_in, 16)
            sp.dma_start(wb[:], w_b).then_inc(weights_in, 16)
            sp.dma_start(x_in[1][:], x[1].rearrange("(t p) d -> p t d", p=P)).then_inc(x_loaded[1], 16)
            sp.dma_start(id_b[:], ident_b).then_inc(consts_in, 16)
            sp.dma_start(mask_b[:], causal).then_inc(consts_in, 16)
            for p in range(2):
                sp.dma_start(q_aug[p][0:NCONST], aug_q[0:NCONST]).then_inc(aug_in, 16)
                sp.dma_start(k_aug[p][0:NCONST], aug_k[0:NCONST]).then_inc(aug_in, 16)
                sp.dma_start(q_aug[p][NCONST + NSPLIT:MROW], aug_q[NCONST:NCONST + MROW - NCONST - NSPLIT])\
                  .then_inc(aug_in, 16)
                sp.dma_start(k_aug[p][NCONST + NSPLIT:KROWS], aug_k[NCONST:]).then_inc(aug_in, 16)

            def m_rows_in(s, g, b):
                p = s % 2
                reach(sp, s1_free, b, s1_at(b, g) + 1, NG * N1)
                dst = q_aug[(s // NG) % 2]
                for r in range(2):
                    sp.dma_start(dst[MROW + r:MROW + r + 1, G * g:G * g + G, :]
                                 .rearrange("o h (i q) -> o (h i) q", q=P),
                                 m_rows[p][G * NT * r:G * NT * (r + 1), :]).then_inc(m_loaded[p], 16)

            def parts_to_dram(b, n):
                p = b % 2
                reach(sp, rest[n], b, 2, 2)
                dram = (q_dram if n == "q" else k_dram)[p]
                for i in range(3):
                    sp.dma_start(dram[:, i], parts[n][:, i, :]).then_inc(parts_out[p], 16)

            def parts_to_rows(b):
                p = b % 2
                sp.wait_ge(parts_out[p], 96 * (b // 2 + 1))
                reach(sp, s2_full, b - 2, NG * N2, NG * N2)
                row = NCONST
                for reps in (3, 2, 1):
                    sp.dma_start(q_aug[p][row:row + HD * reps],
                                 q_dram[p][:, 0:reps].rearrange("h s d t -> (s d) h t")).then_inc(aug_loaded[p], 16)
                    for _ in range(reps):
                        sp.dma_start(k_aug[p][row:row + HD],
                                     k_dram[p][:, 3 - reps].rearrange("h d t -> d h t")).then_inc(aug_loaded[p], 16)
                        row += HD

            def iteration(b):
                for at, s, g, k in slots(b):
                    if k == TURN_AT and live(s):
                        m_rows_in(s, g, b)
                    for n in sequence_at("attention", SP_STEP["parts q"], b, at):
                        parts_to_dram(n, "q")
                    for n in sequence_at("attention", SP_STEP["parts k"], b, at):
                        parts_to_dram(n, "k")
                        parts_to_rows(n)
                    for n in sequence_at("load", SP_STEP["load"], b, at):
                        if n >= 2:
                            reach(sp, x1_ready, n - 2)
                            sp.dma_start(x_in[n % 2][:], x[n].rearrange("(t p) d -> p t d", p=P))\
                              .then_inc(x_loaded[n % 2], 16)
                    for n in sequence_at("ffn2", SP_STEP["store"], b, at):
                        reach(sp, ffn_out["ffn2"], n)
                        sp.dma_start(out[n].rearrange("(t p) d -> p t d", p=P), x_out)\
                          .then_inc(stored[n % 2], 16)

            for b in ITERATIONS:
                iteration(b)
            for p in range(2):
                sp.wait_ge(stored[p], 16 * (B // 2))

        @block.gpsimd
        def _(pool):
            pool.memset(neg_half[:], -0.5).then_inc(pool_set, 1)
            for k in FF:
                pool.memset(xnt[k][:, 0:1], 0.0).then_inc(pool_set, 1)
            pool.memset(ones_f[:], 1.0).then_inc(pool_set, 1)
            for p in range(2):
                pool.memset(v_aug[p][:], 1.0).then_inc(pool_set, 1)

            def normalise(k, b):
                p = b % 2
                reach(pool, stats[k], b, 2, 2)
                pool.tensor_scalar(ve[k][:], mv[k][:, :, 1], 1.0, LN_EPS, ALU.mult, ALU.add).then_inc(norm[k], 1)
                pool.tensor_scalar(nmean[k][:], mv[k][:, :, 0], -1.0, 0.0, ALU.mult, ALU.add).then_inc(norm[k], 1)
                reach(pool, norm[k], b, 2, 4)
                pool.tensor_tensor(rstd[k][:], ve[k][:], neg_half[:], ALU.pow).then_inc(norm[k], 1)
                reach(pool, norm[k], b, 3, 4)
                if k == "ffn1":
                    reach(pool, turned["attention"], b - 1)
                elif k == "attention":
                    reach(pool, turned["ffn1"], b)
                else:
                    reach(pool, turned[k], b - 1)
                for t in range(NT):
                    last = pool.tensor_scalar(xn[k][:, t, :], SRC[k][p][:, t, :], nmean[k][:, t:t + 1],
                                              rstd[k][:, t:t + 1], ALU.add, ALU.mult)
                last.then_inc(norm[k], 1)

            def key_times_table(b):
                reach(pool, k_copied, b)
                reach(pool, scan_steps, b - 1, 1, 3)
                if b == 0:
                    pool.wait_ge(dve_set, DVE_TABLE)
                pool.tensor_tensor(kw[:], k_sb[:], w_table[:], ALU.mult).then_inc(kw_ready, 1)

            def square_u(b):
                reach(pool, scan_steps, b, 3, 3)
                reach(pool, a_ss, b - 1)
                pool.tensor_tensor(usq[:], u[:], u[:], ALU.mult).then_inc(usq_ready, 1)

            def rms_power(b):
                reach(pool, msq_ready, b)
                reach(pool, x1_ready, b - 1)
                pool.tensor_tensor(rrms[:], msq[:], neg_half[:], ALU.pow).then_inc(rrms_ready, 1)

            def token_difference(k, b):
                reach(pool, xt_ready[k], b)
                reach(pool, mixed[k], b - 1, 2, 2)
                if k == "ffn2" and b >= 1:
                    pool.wait_ge(stored[(b - 1) % 2], 16 * ((b - 1) // 2 + 1))
                pool.tensor_tensor(dx[k][:], xnt[k][:, 1:1 + T], xnt[k][:, 0:T], ALU.subtract)\
                    .then_inc(dx_ready[k], 1)

            def square_relu(k, b):
                reach(pool, relu_ready[k], b)
                reach(pool, f_v[k], b - 1)
                pool.tensor_tensor(k_act[k][:], k_relu[k][:], k_relu[k][:], ALU.mult).then_inc(act_ready[k], 1)

            def ffn_residual(k, b):
                p = b % 2
                reach(pool, gated_ready[k], b)
                pool.tensor_tensor(DST[k][p][:], gated[k][:].rearrange("p (t d) -> p t d", t=NT),
                                   SRC[k][p][:], ALU.add).then_inc(ffn_out[k], 1)

            def residual_bias(b):
                p = b % 2
                reach(pool, x3_ready, b - 1)
                if b == 0:
                    pool.wait_ge(dve_set, DVE_BIAS)
                pool.tensor_tensor(x_2b[:], x_2[p][:],
                                   bias_o[:].rearrange("p (o d) -> p o d", o=1).to_broadcast([P, NT, D]),
                                   ALU.add).then_inc(x2b_ready, 1)

            def split_rest(n, b, i):
                reach(pool, cast[n], b, i + 1, 2)
                if i == 0:
                    pool.tensor_tensor(qres[n][:], qf[n][:], parts[n][:, 0, :], ALU.subtract).then_inc(rest[n], 1)
                else:
                    pool.tensor_tensor(parts[n][:, 2, :], qres[n][:], parts[n][:, 1, :], ALU.subtract)\
                        .then_inc(rest[n], 1)

            def mask_diagonal(s, b, g, j):
                reach(pool, exp_done, b, N2 * g + EXPS_OF[j], NG * N2)
                blk = pt[s % 2][:, PT_AT[j]:PT_AT[j] + G * WIDTH[j]].rearrange("p (h q) -> p h q", h=G)[:, :, 0:P]
                pool.affine_select(out=blk, in_=blk, compare_op=ALU.is_ge, fill=0.0, base=0,
                                   pattern=[[0, G], [1, P]], channel_multiplier=-1).then_inc(masked, 1)

            def iteration(b):
                for at, s, g, k in slots(b):
                    for j in range(NT):
                        for slot in due(SLOT_STEP[f"mask {j}"], b, g, k):
                            mask_diagonal(*slot, j)
                    for n in sequence_at("residual bias", POOL_STEP["residual bias"], b, at):
                        residual_bias(n)
                    for n in sequence_at("retention", POOL_STEP["normalise retention"], b, at):
                        normalise("retention", n)
                    for n in sequence_at("retention", POOL_STEP["key times table"], b, at):
                        key_times_table(n)
                    for n in sequence_at("retention", POOL_STEP["square u"], b, at):
                        square_u(n)
                    for n in sequence_at("retention", POOL_STEP["rms power"], b, at):
                        rms_power(n)
                    for n in sequence_at("ffn1", POOL_STEP["normalise ffn1"], b, at):
                        normalise("ffn1", n)
                    for n in sequence_at("ffn1", POOL_STEP["token difference ffn1"], b, at):
                        token_difference("ffn1", n)
                    for n in sequence_at("ffn1", POOL_STEP["square relu ffn1"], b, at):
                        square_relu("ffn1", n)
                    for n in sequence_at("ffn1", POOL_STEP["ffn residual ffn1"], b, at):
                        ffn_residual("ffn1", n)
                    for n in sequence_at("attention", POOL_STEP["normalise attention"], b, at):
                        normalise("attention", n)
                    for n in sequence_at("attention", POOL_STEP["split rest q 0"], b, at):
                        split_rest("q", n, 0)
                    for n in sequence_at("attention", POOL_STEP["split rest q 1"], b, at):
                        split_rest("q", n, 1)
                    for n in sequence_at("attention", POOL_STEP["split rest k 0"], b, at):
                        split_rest("k", n, 0)
                    for n in sequence_at("attention", POOL_STEP["split rest k 1"], b, at):
                        split_rest("k", n, 1)
                    for n in sequence_at("ffn2", POOL_STEP["normalise ffn2"], b, at):
                        normalise("ffn2", n)
                    for n in sequence_at("ffn2", POOL_STEP["token difference ffn2"], b, at):
                        token_difference("ffn2", n)
                    for n in sequence_at("ffn2", POOL_STEP["square relu ffn2"], b, at):
                        square_relu("ffn2", n)
                    for n in sequence_at("ffn2", POOL_STEP["ffn residual ffn2"], b, at):
                        ffn_residual("ffn2", n)

            pool.wait_ge(pool_set, 4)
            for b in ITERATIONS:
                iteration(b)

        @block.scalar
        def _(act):
            act.wait_ge(consts_in, 16 * 9)
            act.activation(dcol[:, 1:2], dcol[:, 0:1], ACT.Exp, scale=-1.0).then_inc(act_set, 1)
            act.wait_ge(dve_set, 3)
            act.activation(dcol[:, 4:5], dcol[:, 3:4], ACT.Ln).then_inc(act_set, 1)
            act.wait_ge(act_set, 2)
            act.activation(w_table[:], w_table[:], ACT.Exp, scale=dcol[:, 4:5]).then_inc(act_set, 1)

            def copy_turned(k, b):
                reach(act, turned[k], b)
                if k in FF:
                    reach(act, mixed[k], b - 1, 2, 2)
                act.activation(xnt[k][:, 1:1 + T], BANK[k][:], ACT.Copy).then_inc(xt_ready[k], 1)

            def copy_k(b):
                reach(act, a_k, b)
                reach(act, kw_ready, b - 1)
                act.activation(k_sb[:], a_bank[:], ACT.Copy).then_inc(k_copied, 1)

            def tanh_r(b):
                reach(act, a_r, b)
                reach(act, scan_steps, b - 1, 3, 3)
                act.activation(r_tanh[:], a_bank[:], ACT.Tanh, scale=0.5).then_inc(a_tanh, 1)

            def ffn_tanh(k, b):
                reach(act, f_r[k], b)
                reach(act, gated_ready[k], b - 1)
                act.activation(f_tanh[k][:], BANK[k][:], ACT.Tanh, scale=0.5).then_inc(f_tanh_ready[k], 1)

            def ffn_relu(k, b):
                reach(act, f_k[k], b)
                reach(act, act_ready[k], b - 1)
                act.activation(k_relu[k][:], BANK[k][:], ACT.Relu).then_inc(relu_ready[k], 1)

            def project_q(b):
                reach(act, b_q, b)
                reach(act, rest["q"], b - 1, 1, 2)
                if b == 0:
                    act.wait_ge(dve_set, DVE_ALL)
                act.activation(qf["q"][:], b_bank[:], ACT.Identity, bias=bq_s[:], scale=float(SCALE))\
                    .then_inc(qf_ready["q"], 1)

            def project_k(b):
                reach(act, b_k, b)
                reach(act, rest["k"], b - 1, 1, 2)
                act.activation(qf["k"][:], b_bank[:], ACT.Identity, bias=bcol[:, 1:2])\
                    .then_inc(qf_ready["k"], 1)

            def exponentials(s, b, g, i):
                j, heads = P2_UNITS[i]
                reach(act, s2_full, b, N2 * g + i + 1, NG * N2)
                if i == 0:
                    reach(act, pv_done, b, NT * (g - 1), NG * NT)
                n = WIDTH[j] * len(heads)
                a = PT_AT[j] + WIDTH[j] * heads[0]
                act.activation(pt[s % 2][:, a:a + n], s2_bank[(g + i) % 2][:, 0:n], ACT.Exp).then_inc(exp_done, 1)

            def copy_o(s, b, g):
                reach(act, pv_done, b, NT * (g + 1), NG * NT)
                reach(act, o_turned, b, g, NG)
                act.activation(o_sb[s % 2][:], o_bank[:], ACT.Copy).then_inc(o_copied, 1)

            def copy_o_t(b):
                reach(act, c_turned, b)
                act.activation(o_t[:], c_bank[:], ACT.Copy).then_inc(ot_ready, 1)

            def iteration(b):
                for at, s, g, k in slots(b):
                    for i in range(N2):
                        for slot in due(SLOT_STEP["second pass"] + i, b, g, k):
                            exponentials(*slot, i)
                    for slot in due(SLOT_STEP["copy o"], b, g, k):
                        copy_o(*slot)
                    for n in sequence_at("retention", ACT_STEP["copy turned retention"], b, at):
                        copy_turned("retention", n)
                    for n in sequence_at("retention", ACT_STEP["copy k"], b, at):
                        copy_k(n)
                    for n in sequence_at("retention", ACT_STEP["tanh r"], b, at):
                        tanh_r(n)
                    for n in sequence_at("ffn1", ACT_STEP["copy turned ffn1"], b, at):
                        copy_turned("ffn1", n)
                    for n in sequence_at("ffn1", ACT_STEP["ffn tanh ffn1"], b, at):
                        ffn_tanh("ffn1", n)
                    for n in sequence_at("ffn1", ACT_STEP["ffn relu ffn1"], b, at):
                        ffn_relu("ffn1", n)
                    for n in sequence_at("attention", ACT_STEP["copy turned attention"], b, at):
                        copy_turned("attention", n)
                    for n in sequence_at("attention", ACT_STEP["project q"], b, at):
                        project_q(n)
                    for n in sequence_at("attention", ACT_STEP["project k"], b, at):
                        project_k(n)
                    for n in sequence_at("ffn2", ACT_STEP["copy o t"], b, at):
                        copy_o_t(n)
                    for n in sequence_at("ffn2", ACT_STEP["copy turned ffn2"], b, at):
                        copy_turned("ffn2", n)
                    for n in sequence_at("ffn2", ACT_STEP["ffn tanh ffn2"], b, at):
                        ffn_tanh("ffn2", n)
                    for n in sequence_at("ffn2", ACT_STEP["ffn relu ffn2"], b, at):
                        ffn_relu("ffn2", n)

            act.wait_ge(pool_set, 3)
            for b in ITERATIONS:
                iteration(b)

        @block.vector
        def _(dve):
            dve.wait_ge(act_set, 1)
            dve.tensor_scalar(dcol[:, 2:3], dcol[:, 1:2], 1.0, None, ALU.add).then_inc(dve_set, 1)
            dve.wait_ge(dve_set, 1)
            dve.reciprocal(dcol[:, 5:6], dcol[:, 2:3]).then_inc(dve_set, 1)
            dve.wait_ge(dve_set, 2)
            dve.tensor_scalar(dcol[:, 3:4], dcol[:, 5:6], 1e-7, None, ALU.max).then_inc(dve_set, 1)
            dve.wait_ge(weights_in, 16 * 3)
            dve.tensor_reduce(bsum[:], bw, AX.X, ALU.add, apply_absolute_value=True).then_inc(bw_set, 1)
            dve.wait_ge(bw_set, 1)
            dve.tensor_scalar(bscale[:], bsum[:], 1.0 / D, 1e-5, ALU.mult, ALU.max).then_inc(bw_set, 1)
            dve.wait_ge(bw_set, 2)
            dve.tensor_scalar(bhalf[:, 0, :], bscale[:], 0.5, None, ALU.mult)
            dve.tensor_scalar(bhalf[:, 1, :], bscale[:], -0.5, None, ALU.mult).then_inc(bw_set, 1)
            dve.wait_ge(bw_set, 3)
            for i in range(4):
                dve.tensor_scalar(bw_gt, bw[:, i, :], bhalf[:, 0, i:i + 1], bscale[:, i:i + 1], ALU.is_gt, ALU.mult)
                dve.tensor_scalar(bw_lt, bw[:, i, :], bhalf[:, 1, i:i + 1], bscale[:, i:i + 1], ALU.is_lt, ALU.mult)\
                    .then_inc(bw_set, 1)
                dve.wait_ge(bw_set, 4 + 4 * i)
                dve.tensor_tensor(bw_q[:, i, :], bw_gt, bw_lt, ALU.subtract).then_inc(bw_set, 1)
                dve.wait_ge(bw_set, 5 + 4 * i)
                dve.tensor_tensor(bw_gt, bw_q[:, i, :], bw[:, i, :], ALU.subtract).then_inc(bw_set, 1)
                dve.wait_ge(bw_set, 6 + 4 * i)
                dve.tensor_tensor(bw_q[:, i, :], bw[:, i, :], bw_gt, ALU.add).then_inc(bw_set, 1)
                dve.wait_ge(bw_set, 7 + 4 * i)
            dve.tensor_scalar(wf[:, 2, :], wf[:, 2, :], 0.5, None, ALU.mult).then_inc(dve_set, 1)
            dve.wait_ge(act_set, 3)
            dve.tensor_scalar(w_table[:], w_table[:], 1.0 / CLIP_SCALE, 1.0, ALU.mult, ALU.min).then_inc(dve_set, 1)
            dve.wait_ge(pe_set, 1)
            dve.wait_ge(consts_in, 16 * 9)
            dve.tensor_copy(wa[:, 0:3, :], a_bank[:, 0:3 * P].rearrange("p (w d) -> p w d", w=3)).then_inc(dve_set, 1)
            dve.tensor_scalar(wa[:, 3, :], a_bank[:, 3 * P:4 * P], lnw[:, 0:1], None, ALU.mult).then_inc(dve_set, 1)
            dve.wait_ge(pool_set, 4)
            dve.tensor_scalar(bv_b[:], ones_f[:], bcol[:, 2:3], None, ALU.mult).then_inc(dve_set, 1)
            dve.tensor_scalar(bq_s[:], bcol[:, 0:1], float(SCALE), None, ALU.mult).then_inc(dve_set, 1)
            dve.wait_ge(pe_set, 2)
            dve.tensor_tensor(bias_o[:], c_bank[:, 0:D], bo_b[:], ALU.add).then_inc(dve_set, 1)

            def statistics(k, b):
                p = b % 2
                wait_source(dve, k, b, p)
                for t in range(NT):
                    last = dve.bn_stats(st[k][:, t, :], SRC[k][p][:, t, :])
                last.then_inc(stats[k], 1)
                reach(dve, stats[k], b, 1, 2)
                reach(dve, norm[k], b - 1, 3, 4)
                for t in range(NT):
                    last = dve.bn_aggr(mv[k][:, t, :], st[k][:, t, :])
                last.then_inc(stats[k], 1)

            def scan_state(b):
                reach(dve, a_v, b)
                reach(dve, kw_ready, b)
                dve.tensor_tensor(kvw[:], a_bank[:], kw[:], ALU.mult).then_inc(scan_steps, 1)
                reach(dve, scan_steps, b, 1, 3)
                dve.tensor_tensor_scan(state[:], dcol[:, 3:4].to_broadcast([P, T]), kvw[:], 0.0, ALU.mult, ALU.add)\
                    .then_inc(scan_steps, 1)

            def gate_state(b):
                reach(dve, a_tanh, b)
                reach(dve, scan_steps, b, 2, 3)
                reach(dve, a_y, b - 1)
                dve.scalar_tensor_tensor(out=u[:], in0=r_tanh[:], scalar=1.0, in1=state[:],
                                         op0=ALU.add, op1=ALU.mult).then_inc(scan_steps, 1)

            def mean_square(b):
                reach(dve, a_ss, b)
                reach(dve, rrms_ready, b - 1)
                dve.tensor_scalar(msq[:], a_bank[:, 0:NT], 1.0 / D, 4.0 * RMS_EPS, ALU.mult, ALU.add)\
                    .then_inc(msq_ready, 1)

            def retention_residual(b):
                p = b % 2
                reach(dve, a_y, b)
                reach(dve, rrms_ready, b)
                for t in range(NT):
                    last = dve.scalar_tensor_tensor(out=x_1[p][:, t, :], in0=a_bank[:, t * P:(t + 1) * P],
                                                    scalar=rrms[:, t:t + 1], in1=x_in[p][:, t, :],
                                                    op0=ALU.mult, op1=ALU.add)
                last.then_inc(x1_ready, 1)

            def mix(k, b):
                reach(dve, dx_ready[k], b)
                reach(dve, f_k[k], b - 1)
                if k == "ffn2":
                    reach(dve, c_y, b)
                for i, dst in enumerate((xr[k], xk[k])):
                    dve.scalar_tensor_tensor(out=dst[:], in0=dx[k][:], scalar=mu_sb[:, i:i + 1],
                                             in1=xnt[k][:, 0:T], op0=ALU.mult, op1=ALU.add).then_inc(mixed[k], 1)

            def gate_ffn(k, b):
                reach(dve, f_v[k], b)
                reach(dve, f_tanh_ready[k], b)
                reach(dve, ffn_out[k], b - 1)
                dve.scalar_tensor_tensor(out=gated[k][:], in0=f_tanh[k][:], scalar=1.0, in1=BANK[k][:],
                                         op0=ALU.add, op1=ALU.mult).then_inc(gated_ready[k], 1)

            def cast_part(n, b, i):
                if i == 0:
                    reach(dve, qf_ready[n], b)
                    if b:
                        dve.wait_ge(parts_out[(b - 1) % 2], 96 * ((b - 1) // 2 + 1))
                    dve.tensor_copy(parts[n][:, 0, :], qf[n][:]).then_inc(cast[n], 1)
                else:
                    reach(dve, rest[n], b, 1, 2)
                    dve.tensor_copy(parts[n][:, 1, :], qres[n][:]).then_inc(cast[n], 1)

            def copy_v(b):
                p = b % 2
                reach(dve, b_v, b)
                reach(dve, pv_done, b - 2, NG * NT, NG * NT)
                if b < 2:
                    dve.wait_ge(pool_set, 6)
                dve.tensor_copy(v_aug[p][:, :, :, 0:HD], b_bank[:].rearrange("p (t h d) -> p t h d", t=NT, h=H))\
                    .then_inc(v_ready, 1)

            def block_maxima(b, g, i):
                nxt = (g + 1) % 2
                unit = P1_UNITS[i]
                h, q = unit[0]
                bank = s1_of(b, g, i)
                reach(dve, s1_full, b, s1_at(b, g, i) + 1, NG * N1)
                if i == 0:
                    reach(dve, mparts_ready, b, 2 * g, 2 * NG)
                if q == 3:
                    dve.tensor_reduce(negm[nxt][:, h, 3:4], bank[:], AX.X, ALU.max, negate=True).then_inc(s1_free, 1)
                elif q == 1:
                    dve.tensor_reduce(negm[nxt][:, h:h + 2, 1:2].rearrange("p h o -> p (h o)"),
                                      bank[:].rearrange("p (h k) -> p h k", h=2),
                                      AX.X, ALU.max, negate=True).then_inc(s1_free, 1)
                else:
                    dve.tensor_reduce(bmax[nxt][:, h, :], bank[:].rearrange("p (j k) -> p j k", j=NT),
                                      AX.X, ALU.max).then_inc(s1_free, 1)

            def group_maxima(b, g):
                nxt = (g + 1) % 2
                reach(dve, s1_free, b, s1_at(b, g, N1 - 2) + 1, NG * N1)
                dve.tensor_reduce(negm[nxt][:, :, 2:3].rearrange("p h o -> p (h o)"), bmax[nxt][:, :, 0:3],
                                  AX.X, ALU.max, negate=True).then_inc(negm_ready, 1)
                dve.tensor_scalar(negm[nxt][:, :, 0], bmax[nxt][:, :, 3], -1.0, None, ALU.mult)\
                    .then_inc(negm_ready, 1)

            def split_max(s, b, g):
                p = s % 2
                reach(dve, negm_ready, b, 2 * g + 2, 2 * NG)
                dve.tensor_copy(m_parts[p][:, 0, :], negm[p][:].rearrange("p h i -> p (h i)"))\
                    .then_inc(mparts_ready, 1)
                reach(dve, mparts_ready, b, 2 * g + 1, 2 * NG)
                dve.tensor_tensor(m_parts[p][:, 1, :], negm[p][:].rearrange("p h i -> p (h i)"),
                                   m_parts[p][:, 0, :], ALU.subtract).then_inc(mparts_ready, 1)

            def copy_max_rows(s, b, g):
                p = s % 2
                reach(dve, s1_full, b, s1_at(b, g) + 1, NG * N1)
                if s >= 2:
                    dve.wait_ge(m_loaded[p], 32 * (s // 2))
                dve.tensor_copy(m_rows[p][:], s1_of(b, g)[0:2 * G * NT, 0:P // 2].bitcast(BF16))\
                    .then_inc(s1_free, 1)

            def normalise_o(s, b, g):
                reach(dve, o_turned, b, g + 1, NG)
                o = o_bank[:].rearrange("p (t h c) -> p t h c", t=NT, h=G)
                dve.reciprocal(rsum[:], o[:, :, :, HD]).then_inc(o_normed, 1)
                reach(dve, o_normed, b, 2 * g + 1, 2 * NG)
                if g == 0:
                    reach(dve, c_turned, b - 1)
                dst = o_tm[(s // NG) % 2][:, :, G * HD * g:G * HD * (g + 1)].rearrange("p t (h d) -> p t h d", h=G)
                dve.tensor_tensor(dst, o[:, :, :, 0:HD],
                                  rsum[:].rearrange("p t (h o) -> p t h o", o=1).to_broadcast([P, NT, G, HD]),
                                  ALU.mult).then_inc(o_normed, 1)

            def attention_residual(b):
                p = b % 2
                reach(dve, c_y, b)
                reach(dve, x2b_ready, b)
                dve.tensor_tensor(x_3[p][:].rearrange("p t d -> p (t d)"), c_bank[:],
                                  x_2b[:].rearrange("p t d -> p (t d)"), ALU.add).then_inc(x3_ready, 1)

            def iteration(b):
                for at, s, g, k in slots(b):
                    for slot in due(SLOT_STEP["normalise o"], b, g, k):
                        normalise_o(*slot)
                    if k < TURN_AT and live(s + 1):
                        block_maxima(b, g, k)
                    if k == 0 and live(s):
                        split_max(s, b, g)
                    if k == TURN_AT and live(s):
                        copy_max_rows(s, b, g)
                    if k > TURN_AT and live(s + 1):
                        block_maxima(b, g, k - 1)
                        if k == STEPS - 1:
                            group_maxima(b, g)
                    for n in sequence_at("retention", DVE_STEP["statistics retention"], b, at):
                        statistics("retention", n)
                    for n in sequence_at("retention", DVE_STEP["scan state"], b, at):
                        scan_state(n)
                    for n in sequence_at("retention", DVE_STEP["gate state"], b, at):
                        gate_state(n)
                    for n in sequence_at("retention", DVE_STEP["mean square"], b, at):
                        mean_square(n)
                    for n in sequence_at("retention", DVE_STEP["retention residual"], b, at):
                        retention_residual(n)
                        statistics("ffn1", n)
                    for n in sequence_at("ffn1", DVE_STEP["mix ffn1"], b, at):
                        mix("ffn1", n)
                    for n in sequence_at("ffn1", DVE_STEP["gate ffn ffn1"], b, at):
                        gate_ffn("ffn1", n)
                    for n in sequence_at("attention", DVE_STEP["statistics attention"], b, at):
                        statistics("attention", n)
                    for n in sequence_at("attention", DVE_STEP["cast part q 0"], b, at):
                        cast_part("q", n, 0)
                    for n in sequence_at("attention", DVE_STEP["copy v"], b, at):
                        copy_v(n)
                    for n in sequence_at("attention", DVE_STEP["cast part k 0"], b, at):
                        cast_part("k", n, 0)
                    for n in sequence_at("attention", DVE_STEP["cast part q 1"], b, at):
                        cast_part("q", n, 1)
                    for n in sequence_at("attention", DVE_STEP["cast part k 1"], b, at):
                        cast_part("k", n, 1)
                    for n in sequence_at("ffn2", DVE_STEP["attention residual"], b, at):
                        attention_residual(n)
                        statistics("ffn2", n)
                    for n in sequence_at("ffn2", DVE_STEP["mix ffn2"], b, at):
                        mix("ffn2", n)
                    for n in sequence_at("ffn2", DVE_STEP["gate ffn ffn2"], b, at):
                        gate_ffn("ffn2", n)

            for b in ITERATIONS:
                iteration(b)

        @block.tensor
        def _(pe):
            pe.wait_ge(consts_in, 16 * 9)
            for i in range(4):
                pe.wait_ge(bw_set, 7 + 4 * i)
                last = pe.transpose(a_bank[:, i * P:(i + 1) * P], bw_q[:, i, :], id_f[:])
            last.then_inc(pe_set, 1)
            pe.wait_ge(dve_set, 9)
            pe.matmul(c_bank[:, 0:D], bv_b[:], wb[:, 3, :], start=True, stop=True).then_inc(pe_set, 1)
            pe.wait_ge(dve_set, DVE_ALL)

            def turn(k, b):
                reach(pe, norm[k], b, 4, 4)
                if k == "retention":
                    reach(pe, x1_ready, b - 1)
                elif k == "ffn1":
                    reach(pe, v_ready, b - 1)
                elif k == "attention":
                    reach(pe, gated_ready["ffn1"], b)
                else:
                    reach(pe, x3_ready, b)
                for t in range(NT):
                    last = pe.transpose(BANK[k][:, t * P:(t + 1) * P], xn[k][:, t, :], id_f[:])
                last.then_inc(turned[k], 1)

            def to_channels(bank, weight, src, signal):
                pe.matmul(bank[:], weight, src, start=True, stop=True).then_inc(signal, 1)

            def to_tokens(bank, src, weight, signal):
                for t in range(NT):
                    last = pe.matmul(bank[:, t * P:(t + 1) * P], src[:, t * P:(t + 1) * P], weight,
                                     start=True, stop=True)
                last.then_inc(signal, 1)

            def retention_k(b):
                reach(pe, xt_ready["retention"], b)
                to_channels(a_bank, wa[:, 1, :], xnt["retention"][:, 1:1 + T], a_k)

            def retention_r(b):
                reach(pe, k_copied, b)
                to_channels(a_bank, wa[:, 0, :], xnt["retention"][:, 1:1 + T], a_r)

            def retention_v(b):
                reach(pe, a_tanh, b)
                to_channels(a_bank, wa[:, 2, :], xnt["retention"][:, 1:1 + T], a_v)

            def sum_squares(b):
                reach(pe, usq_ready, b)
                reach(pe, scan_steps, b, 1, 3)
                for t in range(NT):
                    last = pe.matmul(a_bank[:, t:t + 1], usq[:, t * P:(t + 1) * P], ones_f[:, 0:1],
                                     start=True, stop=True)
                last.then_inc(a_ss, 1)

            def retention_out(b):
                reach(pe, msq_ready, b)
                reach(pe, scan_steps, b, 3, 3)
                to_tokens(a_bank, u, wa[:, 3, :], a_y)

            def ffn_r(k, b):
                reach(pe, mixed[k], b, 1, 2)
                to_tokens(BANK[k], xr[k], wf[:, 0, :], f_r[k])

            def ffn_k(k, b):
                reach(pe, mixed[k], b, 2, 2)
                reach(pe, f_tanh_ready[k], b)
                to_channels(BANK[k], wf[:, 1, :], xk[k][:], f_k[k])

            def ffn_v(k, b):
                reach(pe, act_ready[k], b)
                to_tokens(BANK[k], k_act[k], wf[:, 2, :], f_v[k])

            def attention_q(b):
                reach(pe, xt_ready["attention"], b)
                to_channels(b_bank, wb[:, 0, :], xnt["attention"][:, 1:1 + T], b_q)

            def attention_k(b):
                reach(pe, qf_ready["q"], b)
                to_channels(b_bank, wb[:, 1, :], xnt["attention"][:, 1:1 + T], b_k)

            def attention_v(b):
                reach(pe, qf_ready["k"], b)
                to_tokens(b_bank, xnt["attention"][:, 1:1 + T], wb[:, 2, :], b_v)

            def first_pass(b, g, i):
                nb, ng = (b, g + 1) if g + 1 < NG else (b + 1, 0)
                p = nb % 2
                if ng == 0 and i == 0:
                    pe.wait_ge(aug_loaded[p], 16 * 9 * (nb // 2 + 1))
                    if nb < 2:
                        pe.wait_ge(aug_in, 16 * 8)
                bank = s1_of(b, g, i)
                reach(pe, s1_free, b, s1_at(b, g, i) - 1, NG * N1)
                col = 0
                for h, q in P1_UNITS[i]:
                    n = P * (q + 1)
                    head = G * ng + h
                    pe.matmul(bank[:, col:col + n], q_aug[p][0:MROW, head, q * P:(q + 1) * P],
                              k_aug[p][0:MROW, head, 0:n], start=True, stop=False)
                    last = pe.matmul(bank[:, col + n - P:col + n], id_b[:], mask_b[:], start=False, stop=True)
                    col += n
                last.then_inc(s1_full, 1)

            def turn_maxima(s, b, g):
                reach(pe, mparts_ready, b, 2 * g + 2, 2 * NG)
                reach(pe, s1_free, b, s1_at(b, g) - 1, NG * N1)
                pe.transpose(s1_of(b, g)[0:2 * G * NT, 0:P // 2].bitcast(BF16),
                             m_parts[s % 2][:].rearrange("p a m -> p (a m)"), id_b[:]).then_inc(s1_full, 1)

            def second_pass(s, b, g, i):
                j, heads = P2_UNITS[i]
                p = (s // NG) % 2
                if i == 0:
                    pe.wait_ge(m_loaded[s % 2], 32 * (s // 2 + 1))
                reach(pe, exp_done, b, N2 * g + i - 1, NG * N2)
                w = WIDTH[j]
                for c, h in enumerate(heads):
                    last = pe.matmul(s2_bank[(g + i) % 2][:, c * w:(c + 1) * w],
                                     k_aug[p][0:KROWS, G * g + h, j * P:(j + 1) * P],
                                     q_aug[p][0:KROWS, G * g + h, j * P:T], start=True, stop=True)
                last.then_inc(s2_full, 1)

            def weigh_values(s, b, g, j):
                p = (s // NG) % 2
                reach(pe, masked, b, NT * g + j + 1, NG * NT)
                if j == 0:
                    reach(pe, o_normed, b, 2 * g, 2 * NG)
                    if g == 0:
                        reach(pe, v_ready, b)
                w = WIDTH[j]
                for h in range(G):
                    a = PT_AT[j] + w * h
                    last = pe.matmul(o_bank[VW * h:VW * (h + 1), j * P:T], v_aug[p][:, j, G * g + h, :],
                                     pt[s % 2][:, a:a + w], start=(j == 0), stop=(j == NT - 1))
                last.then_inc(pv_done, 1)

            def turn_o(s, b, g):
                reach(pe, o_copied, b, g + 1, NG)
                for t in range(NT):
                    last = pe.transpose(o_bank[:, t * P:(t + 1) * P], o_sb[s % 2][:, t * P:(t + 1) * P], id_f[:])
                last.then_inc(o_turned, 1)

            def turn_heads(b):
                reach(pe, o_normed, b, 2 * NG, 2 * NG)
                reach(pe, gated_ready["ffn2"], b - 1)
                for t in range(NT):
                    last = pe.transpose(c_bank[:, t * P:(t + 1) * P], o_tm[b % 2][:, t, :], id_f[:])
                last.then_inc(c_turned, 1)

            def attention_out(b):
                reach(pe, ot_ready, b)
                to_tokens(c_bank, o_t, wb[:, 3, :], c_y)

            def iteration(b):
                for at, s, g, k in slots(b):
                    if k == TURN_AT and live(s):
                        turn_maxima(s, b, g)
                    elif k != TURN_AT and live(s + 1):
                        first_pass(b, g, k if k < TURN_AT else k - 1)
                    for i in range(N2):
                        for slot in due(SLOT_STEP["second pass"] + i, b, g, k):
                            second_pass(*slot, i)
                    for j in range(NT):
                        for slot in due(SLOT_STEP[f"weigh values {j}"], b, g, k):
                            weigh_values(*slot, j)
                    for slot in due(SLOT_STEP["turn o"], b, g, k):
                        turn_o(*slot)
                    for n in sequence_at("retention", PE_STEP["turn retention"], b, at):
                        turn("retention", n)
                    for n in sequence_at("retention", PE_STEP["retention k"], b, at):
                        retention_k(n)
                    for n in sequence_at("retention", PE_STEP["retention r"], b, at):
                        retention_r(n)
                    for n in sequence_at("retention", PE_STEP["retention v"], b, at):
                        retention_v(n)
                    for n in sequence_at("retention", PE_STEP["sum squares"], b, at):
                        sum_squares(n)
                    for n in sequence_at("retention", PE_STEP["retention out"], b, at):
                        retention_out(n)
                    for n in sequence_at("ffn1", PE_STEP["turn ffn1"], b, at):
                        turn("ffn1", n)
                    for n in sequence_at("ffn1", PE_STEP["ffn r ffn1"], b, at):
                        ffn_r("ffn1", n)
                    for n in sequence_at("ffn1", PE_STEP["ffn k ffn1"], b, at):
                        ffn_k("ffn1", n)
                    for n in sequence_at("ffn1", PE_STEP["ffn v ffn1"], b, at):
                        ffn_v("ffn1", n)
                    for n in sequence_at("attention", PE_STEP["turn attention"], b, at):
                        turn("attention", n)
                    for n in sequence_at("attention", PE_STEP["attention q"], b, at):
                        attention_q(n)
                    for n in sequence_at("attention", PE_STEP["attention k"], b, at):
                        attention_k(n)
                    for n in sequence_at("attention", PE_STEP["attention v"], b, at):
                        attention_v(n)
                    for n in sequence_at("ffn2", PE_STEP["turn heads"], b, at):
                        turn_heads(n)
                    for n in sequence_at("ffn2", PE_STEP["attention out"], b, at):
                        attention_out(n)
                    for n in sequence_at("ffn2", PE_STEP["turn ffn2"], b, at):
                        turn("ffn2", n)
                    for n in sequence_at("ffn2", PE_STEP["ffn r ffn2"], b, at):
                        ffn_r("ffn2", n)
                    for n in sequence_at("ffn2", PE_STEP["ffn k ffn2"], b, at):
                        ffn_k("ffn2", n)
                    for n in sequence_at("ffn2", PE_STEP["ffn v ffn2"], b, at):
                        ffn_v("ffn2", n)

            for b in ITERATIONS:
                iteration(b)


def bf16_parts(a, n):
    out = []
    for _ in range(n):
        part = a.astype(mybir.dt.np(BF16))
        out.append(part)
        a = (a - part.astype(np.float32)).astype(np.float32)
    return out


def constants():
    bf = mybir.dt.np(BF16)
    slope = np.power(np.float32(2.0), (-8.0 * np.arange(1, H + 1) / H).astype(np.float32)).astype(np.float32)
    token = np.arange(T)
    lo, hi = (token % 256).astype(bf), (token - token % 256).astype(bf)
    aug_q = np.zeros((KROWS - NSPLIT, H, T), bf)
    aug_k = np.zeros((KROWS - NSPLIT, H, T), bf)
    aug_k[MROW - NSPLIT:] = 1.0
    for i, s in enumerate(bf16_parts(slope, 3)):
        aug_q[4 * i] = aug_q[4 * i + 1] = s[:, None]
        aug_k[4 * i], aug_k[4 * i + 1] = lo, hi
        aug_q[4 * i + 2], aug_q[4 * i + 3] = lo, hi
        aug_k[4 * i + 2] = aug_k[4 * i + 3] = -s[:, None]
    for r in range(1, T // SUB):
        aug_k[NBIAS + r - 1] = (token // SUB == r).astype(bf)
        aug_q[NBIAS + r - 1] = np.where(token // SUB < r, np.float32(FAR), np.float32(0)).astype(bf)
    causal = np.where(np.arange(P)[None, :] > np.arange(P)[:, None], np.float32(FAR), np.float32(0)).astype(bf)
    return {
        "ident": np.eye(P, dtype=np.float32), "ident_b": np.eye(P, dtype=np.float32).astype(bf), "causal": causal,
        "pos": np.broadcast_to(np.arange(T, dtype=np.float32), (P, T)).copy(), "aug_q": aug_q, "aug_k": aug_k,
    }


def kernel(**inputs):
    import concourse.bacc as _bacc
    from concourse.bass_utils import run_bass_kernel_spmd as _run

    a = {k: np.asarray(v) for k, v in inputs.items()}

    def col(*names):
        return np.ascontiguousarray(np.stack([a[n] for n in names], axis=1))

    arrays = {
        "x": np.ascontiguousarray(a["L0_attn_a_x"]),
        "w_a": np.ascontiguousarray(np.stack([a[f"L0_attn_a_W{n}"] for n in "rkvo"], axis=1)),
        "w_f": np.ascontiguousarray(np.stack([a[f"L0_ffn_W_{n}"].T for n in "rkv"], axis=1)),
        "w_b": np.ascontiguousarray(np.stack([a[f"L0_attn_b_W{n}"].T for n in "qkvo"], axis=1)),
        "decay": col("L0_attn_a_decay"), "ln_w": col("L0_attn_a_ln_w"),
        "mu": col("L0_ffn_mu_r", "L0_ffn_mu_k"),
        "b_cols": col("L0_attn_b_bq", "L0_attn_b_bk", "L0_attn_b_bv"),
        "bo_row": np.ascontiguousarray(a["L0_attn_b_bo"].reshape(1, D)),
        **constants(),
    }
    nc = _bacc.Bacc("TRN2", target_bir_lowering=False, num_devices=1)
    args = {k: nc.dram_tensor(k, v.shape, mybir.dt.from_np(v.dtype), kind="ExternalInput").ap()
            for k, v in arrays.items()}
    args["out"] = nc.dram_tensor("out", (B, T, D), F32, kind="ExternalOutput").ap()
    build(nc, **args)
    r = _run(nc, [arrays], core_ids=[0])
    return r.results[0]["out"]
```

```python
from contextlib import ExitStack

import numpy as np

import concourse.bass as bass
from concourse import mybir

F32 = mybir.dt.float32
BF16 = mybir.dt.bfloat16
ACT = mybir.ActivationFunctionType
ALU = mybir.AluOpType
AX = mybir.AxisListType

P = 128
B = 8
T = 512
NT = T // P
D = 128
H = 16
HD = D // H
G = 4
NG = H // G
VW = 32
SCALE = 1.0 / np.sqrt(HD)
LN_EPS = 1e-5
RMS_EPS = 1e-6
CLIP_SCALE = 1e-10

SUB = 16
NBIAS = 12
NCONST = NBIAS + T // SUB - 1
FAR = -1e30
NSPLIT = 6 * HD
MROW = 96
KROWS = MROW + 2

WIDTH = [T - P * j for j in range(NT)]
PT_AT = [G * sum(WIDTH[:j]) for j in range(NT)]
PT_COLS = G * sum(WIDTH)

P1_UNITS = [[(h, 3)] for h in range(G)] + [[(0, 1), (1, 1)], [(2, 1), (3, 1)]] + [[(h, 2), (h, 0)] for h in range(G)]
P2_UNITS = [(0, [h]) for h in range(G)] + [(1, [h]) for h in range(G)] + [(2, [0, 1]), (2, [2, 3]), (3, [0, 1, 2, 3])]
N1, N2 = len(P1_UNITS) + 1, len(P2_UNITS)
STEPS = 11
EXPS_OF = [sum(1 for j, _ in P2_UNITS if j <= jj) for jj in range(NT)]
TURN_AT = 3

SLOT_STEP = {
    "second pass": 7,
    "mask 0": 10,
    "mask 1": 13,
    "mask 2": 14,
    "mask 3": 16,
    "weigh values 0": 14,
    "weigh values 1": 17,
    "weigh values 2": 20,
    "weigh values 3": 20,
    "copy o": 20,
    "turn o": 22,
    "normalise o": 23,
}

SP_STEP = {
    "parts q": 6,
    "parts k": 21,
    "load": 26,
    "store": 38,
}
DELAY_STEP = {
    "retention 0": -37,
    "retention 1": -53,
    "retention 2": 0,
    "ffn1 0": -28,
    "ffn1 1": -13,
    "ffn1 2": 3,
    "attention 0": 0,
    "attention 1": 0,
    "attention 2": -1,
    "ffn2 5": 1,
    "ffn2 6": 1,
    "ffn2 7": 20,
}
POOL_STEP = {
    "residual bias": 22,
    "normalise retention": 2,
    "key times table": 7,
    "rms power": 18,
    "normalise ffn1": 20,
    "token difference ffn1": 23,
    "ffn residual ffn1": 38,
    "normalise attention": 1,
    "split rest q 0": 5,
    "split rest q 1": 8,
    "split rest k 0": 11,
    "split rest k 1": 15,
    "normalise ffn2": 18,
    "token difference ffn2": 21,
    "ffn residual ffn2": 32,
}
ACT_STEP = {
    "copy turned retention": 6,
    "copy k": 8,
    "tanh r": 11,
    "square u": 16,
    "copy turned ffn1": 23,
    "ffn tanh ffn1": 30,
    "ffn relu ffn1": 31,
    "square relu ffn1": 31,
    "copy turned attention": 3,
    "project q": 5,
    "project k": 6,
    "copy o t": 13,
    "copy turned ffn2": 22,
    "ffn tanh ffn2": 27,
    "ffn relu ffn2": 29,
    "square relu ffn2": 29,
}
DVE_STEP = {
    "statistics retention": 1,
    "scan state": 12,
    "gate state": 15,
    "mean square": 16,
    "retention residual": 18,
    "mix ffn1": 27,
    "gate ffn ffn1": 36,
    "statistics attention": 0,
    "cast part q 0": 5,
    "copy v": 9,
    "cast part k 0": 9,
    "cast part q 1": 10,
    "cast part k 1": 13,
    "attention residual": 15,
    "mix ffn2": 26,
    "gate ffn ffn2": 31,
}
PE_STEP = {
    "turn retention": 6,
    "retention k": 7,
    "retention r": 11,
    "retention v": 13,
    "sum squares": 17,
    "retention out": 19,
    "turn ffn1": 24,
    "ffn r ffn1": 29,
    "ffn k ffn1": 32,
    "ffn v ffn1": 34,
    "turn attention": 4,
    "attention q": 5,
    "attention k": 6,
    "attention v": 9,
    "turn heads": 13,
    "attention out": 15,
    "turn ffn2": 22,
    "ffn r ffn2": 27,
    "ffn k ffn2": 29,
    "ffn v ffn2": 31,
}


def build(nc, x, w_a, w_f, w_b, decay, ln_w, mu, b_cols, bo_row, ident, ident_b, causal, pos, aug_q, aug_k, out):
    ctx = ExitStack()
    with ctx:
        def sb(name, shape, dt=F32):
            return ctx.enter_context(nc.sbuf_tensor(name, shape, dt))

        def ps(name):
            return ctx.enter_context(nc.psum_tensor(name, [P, T], F32))

        def sem(name):
            return ctx.enter_context(nc.semaphore(name))

        s1_bank = [ps(f"s1_bank{p}") for p in range(3)]
        s2_bank = [ps("s2_bank0"), ps("s2_bank1")]
        o_bank = ps("o_bank")
        a_bank = ps("a_bank")
        c_bank = ps("c_bank")

        id_f = sb("id_f", [P, P])
        id_b = sb("id_b", [P, P], BF16)
        mask_b = sb("mask_b", [P, P], BF16)
        w_table = sb("w_table", [P, T])
        bsum = sb("bsum", [P, 4])
        bscale = sb("bscale", [P, 4])
        bhalf = sb("bhalf", [P, 2, 4])
        wa = sb("wa", [P, 4, P])
        wf = sb("wf", [P, 3, P])
        wb = sb("wb", [P, 4, P])
        dcol = sb("dcol", [P, 6])
        lnw = sb("lnw", [P, 1])
        mu_sb = sb("mu_sb", [P, 2])
        bcol = sb("bcol", [P, 3])
        bq_s = sb("bq_s", [P, 1])
        ones_f = sb("ones_f", [P, P])
        bv_b = sb("bv_b", [P, P])
        bo_b = sb("bo_b", [P, P])
        bias_o = sb("bias_o", [P, P])
        neg_half = sb("neg_half", [P, NT])

        x_in = [sb(f"x_in{p}", [P, NT, D]) for p in range(2)]
        x_1 = [sb("x_1", [P, NT, D])] * 2
        x_2 = [sb(f"x_2{p}", [P, NT, D]) for p in range(2)]
        x_2b = sb("x_2b", [P, NT, D])
        x_3 = [sb("x_3", [P, NT, D])] * 2
        LN = ["retention", "ffn1", "attention", "ffn2"]
        st = {k: sb(f"st_{k}", [P, NT, 6]) for k in LN}
        mv = {k: sb(f"mv_{k}", [P, NT, 2]) for k in LN}
        ve = {k: sb(f"ve_{k}", [P, NT]) for k in LN}
        rstd = {k: sb(f"rstd_{k}", [P, NT]) for k in LN}
        nmean = {k: sb(f"nmean_{k}", [P, NT]) for k in LN}
        xn = {k: sb(f"xn_{k}", [P, NT, D]) for k in LN if k != "attention"}
        xn["attention"] = xn["ffn1"]
        xnt = {k: sb(f"xnt_{k}", [P, 1 + T]) for k in LN}

        k_sb = sb("k_sb", [P, T])
        kw = sb("kw", [P, T])
        kvw = sb("kvw", [P, T])
        state = k_sb
        r_tanh = sb("r_tanh", [P, T])
        u = kvw
        usq = kw
        msq = sb("msq", [P, NT])
        rrms = sb("rrms", [P, NT])

        FF = ["ffn1", "ffn2"]
        dx = {k: sb(f"dx_{k}", [P, T]) for k in FF}
        xr = {k: sb(f"xr_{k}", [P, T]) for k in FF}
        xk = {k: sb(f"xk_{k}", [P, T]) for k in FF}
        f_tanh = {k: sb(f"f_tanh_{k}", [P, T]) for k in FF}
        k_relu = {k: sb(f"k_relu_{k}", [P, T]) for k in FF}
        k_act = k_relu
        gated = dx
        x_out = dx["ffn2"][:].rearrange("p (t d) -> p t d", t=NT)

        qf = {n: sb(f"{n}f", [P, T]) for n in "qk"}
        qres = {n: sb(f"{n}res", [P, T]) for n in "qk"}
        parts = {n: sb(f"{n}parts", [P, 3, T], BF16) for n in "qk"}
        q_aug = [sb(f"q_aug{p}", [P, H, T], BF16) for p in range(2)]
        k_aug = [sb(f"k_aug{p}", [P, H, T], BF16) for p in range(2)]
        v_aug = [sb(f"v_aug{p}", [P, NT, H, VW]) for p in range(2)]
        q_dram = [nc.dram_tensor(f"q_dram{p}", [H, 3, HD, T], BF16, kind="Internal").ap() for p in range(2)]
        k_dram = [nc.dram_tensor(f"k_dram{p}", [H, 3, HD, T], BF16, kind="Internal").ap() for p in range(2)]

        bmax = [sb(f"bmax{p}", [P, G, NT]) for p in range(2)]
        negm = [sb(f"negm{p}", [P, G, NT]) for p in range(2)]
        m_parts = [sb(f"m_parts{p}", [P, 2, G * NT], BF16) for p in range(2)]
        m_rows = [sb(f"m_rows{p}", [2 * G * NT, P], BF16) for p in range(2)]
        pt = [sb(f"pt{p}", [P, PT_COLS]) for p in range(2)]
        bw = pt[1][:, 0:4 * P].rearrange("p (w c) -> p w c", w=4)
        bw_q = pt[1][:, 4 * P:8 * P].rearrange("p (w c) -> p w c", w=4)
        bw_gt = pt[1][:, 8 * P:12 * P].rearrange("p (w c) -> p w c", w=4)
        bw_lt = pt[1][:, 12 * P:16 * P].rearrange("p (w c) -> p w c", w=4)
        o_sb = [sb("o_sb", [P, T])] * 2
        rsum = sb("rsum", [P, NT, G])
        o_tm = [sb("o_tm", [P, NT, D])] * 2
        o_t = xr["ffn2"]

        ident_in, table_in, cols_in, masks_in = (sem(n) for n in ("ident_in", "table_in", "cols_in", "masks_in"))
        bw_in, weights_in, aug_in = sem("bw_in"), sem("weights_in"), sem("aug_in")
        fills, ones_set = sem("fills"), sem("ones_set")
        decay_steps, table_steps = sem("decay_steps"), sem("table_steps")
        bw_steps, bw_turned, wa_ready = sem("bw_steps"), sem("bw_turned"), sem("wa_ready")
        bv_ready, bq_ready, bias_product = sem("bv_ready"), sem("bq_ready"), sem("bias_product")
        bias_ready, wf_ready = sem("bias_ready"), sem("wf_ready")
        x_loaded = [sem(f"x_loaded{p}") for p in range(2)]
        stored = [sem(f"stored{p}") for p in range(2)]
        stats = {k: sem(f"stats_{k}") for k in LN}
        norm = {k: sem(f"norm_{k}") for k in LN}
        turned = {k: sem(f"turned_{k}") for k in LN}
        xt_ready = {k: sem(f"xt_{k}") for k in LN}
        a_k, a_r, a_v, a_ss, a_y = (sem(n) for n in ("a_k", "a_r", "a_v", "a_ss", "a_y"))
        k_copied, a_tanh, kw_ready, usq_ready, rrms_ready = (
            sem(n) for n in ("k_copied", "a_tanh", "kw_ready", "usq_ready", "rrms_ready"))
        scan_steps = sem("scan_steps")
        msq_ready = sem("msq_ready")
        x1_ready = sem("x1_ready")
        dx_ready = {k: sem(f"dx_{k}_ready") for k in FF}
        mixed = {k: sem(f"mixed_{k}") for k in FF}
        f_r = {k: sem(f"f_r_{k}") for k in FF}
        f_k = {k: sem(f"f_k_{k}") for k in FF}
        f_v = {k: sem(f"f_v_{k}") for k in FF}
        f_tanh_ready = {k: sem(f"f_tanh_ready_{k}") for k in FF}
        relu_ready = {k: sem(f"relu_ready_{k}") for k in FF}
        act_ready = {k: sem(f"act_ready_{k}") for k in FF}
        gated_ready = {k: sem(f"gated_ready_{k}") for k in FF}
        ffn_out = {k: sem(f"ffn_out_{k}") for k in FF}
        x2b_ready = sem("x2b_ready")
        b_q, b_k, b_v = sem("b_q"), sem("b_k"), sem("b_v")
        qf_ready = {n: sem(f"{n}f_ready") for n in "qk"}
        cast = {n: sem(f"{n}_cast") for n in "qk"}
        rest = {n: sem(f"{n}_rest") for n in "qk"}
        v_ready = sem("v_ready")
        parts_out = [sem(f"parts_out{p}") for p in range(2)]
        aug_loaded = [sem(f"aug_loaded{p}") for p in range(2)]
        s1_full, s1_free = sem("s1_full"), sem("s1_free")
        negm_ready = sem("negm_ready")
        mparts_ready = sem("mparts_ready")
        m_loaded = [sem(f"m_loaded{p}") for p in range(2)]
        s2_full, exp_done = sem("s2_full"), sem("exp_done")
        masked, pv_done = sem("masked"), sem("pv_done")
        o_copied, o_turned = sem("o_copied"), sem("o_turned")
        o_normed = sem("o_normed")
        c_turned, ot_ready, c_y, x3_ready = sem("c_turned"), sem("ot_ready"), sem("c_y"), sem("x3_ready")

        def bank_of(k, b):
            return c_bank if k in ("attention", "ffn2") or (k, b) == ("retention", 1) else a_bank

        SRC = {"retention": x_in, "ffn1": x_1, "attention": x_2, "ffn2": x_3}
        DST = {"ffn1": x_2, "ffn2": [x_out, x_out]}

        def reach(eng, s, b, k=1, n=1):
            v = n * b + k
            if isinstance(v, int) and v <= 0:
                return
            eng.wait_ge(s, v)

        def wait_source(eng, k, b, p):
            if k == "retention":
                eng.wait_ge(x_loaded[p], 16 * (b // 2 + 1))
            elif k == "ffn1":
                reach(eng, x1_ready, b)
            elif k == "attention":
                reach(eng, ffn_out["ffn1"], b)
            else:
                reach(eng, x3_ready, b)

        block = ctx.enter_context(nc.Block())

        ITERATIONS = range(-3, B + 2)
        LEAD = {"retention": 2, "ffn1": 2, "attention": 1, "ffn2": -1, "residual bias": 0, "load": 4}

        def s1_turn(b, g, i):
            if i is None:
                return 0 if (b, g) == (B - 1, NG - 1) else TURN_AT
            return i if i < TURN_AT and b >= 0 else i + 1

        def s1_at(b, g, i=None):
            return N1 * g + N1 - 1 + s1_turn(b, g, i)

        def s1_of(b, g, i=None):
            return s1_bank[(NG * N1 * b + s1_at(b, g, i)) % 3]

        def slots(b):
            for at in range(NG * STEPS):
                g, k = divmod(at, STEPS)
                yield at, NG * b + g, g, k

        def live(s):
            return 0 <= s < NG * B

        def sequence_at(stage, offset, b, at):
            for n in range(B):
                late = DELAY_STEP.get(f"{stage} {n}", 0)
                if NG * STEPS * (n - LEAD[stage]) + offset + late == NG * STEPS * b + at:
                    yield n

        def due(offset, b, g, k):
            d, step = divmod(offset, STEPS)
            if k == step and live(NG * b + g - d):
                yield NG * b + g - d, b + (g - d) // NG, (g - d) % NG

        @block.sync
        def _(sp):
            sp.dma_start(x_in[0][:], x[0].rearrange("(t p) d -> p t d", p=P)).then_inc(x_loaded[0], 16)
            sp.dma_start(id_f[:], ident).then_inc(ident_in, 16)
            sp.dma_start(bo_b[:], bo_row.to_broadcast([P, D])).then_inc(cols_in, 16)
            sp.dma_start(mu_sb[:], mu).then_inc(cols_in, 16)
            sp.dma_start(wf[:], w_f).then_inc(weights_in, 16)
            sp.dma_start(x_in[1][:], x[1].rearrange("(t p) d -> p t d", p=P)).then_inc(x_loaded[1], 16)
            sp.dma_start(wb[:], w_b).then_inc(weights_in, 16)
            sp.dma_start(id_b[:], ident_b).then_inc(masks_in, 16)
            sp.dma_start(mask_b[:], causal).then_inc(masks_in, 16)
            for p in range(2):
                sp.dma_start(q_aug[p][0:NCONST], aug_q[0:NCONST]).then_inc(aug_in, 16)
                sp.dma_start(k_aug[p][0:NCONST], aug_k[0:NCONST]).then_inc(aug_in, 16)
                sp.dma_start(q_aug[p][NCONST + NSPLIT:MROW], aug_q[NCONST:NCONST + MROW - NCONST - NSPLIT])\
                  .then_inc(aug_in, 16)
                sp.dma_start(k_aug[p][NCONST + NSPLIT:KROWS], aug_k[NCONST:]).then_inc(aug_in, 16)

            def m_rows_in(s, g, b):
                p = s % 2
                reach(sp, s1_free, b, s1_at(b, g) + 1, NG * N1)
                dst = q_aug[(s // NG) % 2]
                for r in range(2):
                    sp.dma_start(dst[MROW + r:MROW + r + 1, G * g:G * g + G, :]
                                 .rearrange("o h (i q) -> o (h i) q", q=P),
                                 m_rows[p][G * NT * r:G * NT * (r + 1), :]).then_inc(m_loaded[p], 16)

            def parts_to_dram(b, n):
                p = b % 2
                dram = (q_dram if n == "q" else k_dram)[p]
                for i in range(3):
                    reach(sp, *((cast[n], b, i + 1, 2) if i < 2 else (rest[n], b, 2, 2)))
                    sp.dma_start(dram[:, i], parts[n][:, i, :]).then_inc(parts_out[p], 16)

            def parts_to_rows(b):
                p = b % 2
                sp.wait_ge(parts_out[p], 96 * (b // 2 + 1))
                reach(sp, s2_full, b - 2, NG * N2, NG * N2)
                row = NCONST
                for reps in (3, 2, 1):
                    sp.dma_start(q_aug[p][row:row + HD * reps],
                                 q_dram[p][:, 0:reps].rearrange("h s d t -> (s d) h t")).then_inc(aug_loaded[p], 16)
                    for _ in range(reps):
                        sp.dma_start(k_aug[p][row:row + HD],
                                     k_dram[p][:, 3 - reps].rearrange("h d t -> d h t")).then_inc(aug_loaded[p], 16)
                        row += HD

            def iteration(b):
                for at, s, g, k in slots(b):
                    if k == TURN_AT and live(s):
                        m_rows_in(s, g, b)
                    for n in sequence_at("attention", SP_STEP["parts q"], b, at):
                        parts_to_dram(n, "q")
                    for n in sequence_at("attention", SP_STEP["parts k"], b, at):
                        parts_to_dram(n, "k")
                        parts_to_rows(n)
                    for n in sequence_at("load", SP_STEP["load"], b, at):
                        if n >= 2:
                            reach(sp, x1_ready, n - 2)
                            sp.dma_start(x_in[n % 2][:], x[n].rearrange("(t p) d -> p t d", p=P))\
                              .then_inc(x_loaded[n % 2], 16)
                    for n in sequence_at("ffn2", SP_STEP["store"], b, at):
                        reach(sp, ffn_out["ffn2"], n)
                        sp.dma_start(out[n].rearrange("(t p) d -> p t d", p=P), x_out)\
                          .then_inc(stored[n % 2], 16)

            for b in ITERATIONS:
                iteration(b)
            for p in range(2):
                sp.wait_ge(stored[p], 16 * (B // 2))

        @block.gpsimd
        def _(pool):
            pool.memset(neg_half[:], -0.5).then_inc(fills, 1)
            for k in FF:
                pool.memset(xnt[k][:, 0:1], 0.0).then_inc(fills, 1)
            pool.memset(ones_f[:], 1.0).then_inc(fills, 1)
            pool.memset(v_aug[1][:], 1.0).then_inc(ones_set, 1)

            def attention_biases():
                pool.wait_ge(cols_in, 16 * 4)
                pool.tensor_scalar(bv_b[:], ones_f[:], bcol[:, 2:3], 0.0, ALU.mult, ALU.add).then_inc(bv_ready, 1)
                pool.tensor_scalar(bq_s[:], bcol[:, 0:1], float(SCALE), 0.0, ALU.mult, ALU.add).then_inc(bq_ready, 1)

            def normalise(k, b):
                p = b % 2
                reach(pool, stats[k], b, 2, 2)
                pool.tensor_scalar(ve[k][:], mv[k][:, :, 1], 1.0, LN_EPS, ALU.mult, ALU.add).then_inc(norm[k], 1)
                pool.tensor_scalar(nmean[k][:], mv[k][:, :, 0], -1.0, 0.0, ALU.mult, ALU.add).then_inc(norm[k], 1)
                reach(pool, norm[k], b, 2, 4)
                pool.tensor_tensor(rstd[k][:], ve[k][:], neg_half[:], ALU.pow).then_inc(norm[k], 1)
                reach(pool, norm[k], b, 3, 4)
                if k == "ffn1":
                    reach(pool, turned["attention"], b - 1)
                elif k == "attention":
                    reach(pool, turned["ffn1"], b)
                else:
                    reach(pool, turned[k], b - 1)
                for t in range(NT):
                    last = pool.tensor_scalar(xn[k][:, t, :], SRC[k][p][:, t, :], nmean[k][:, t:t + 1],
                                              rstd[k][:, t:t + 1], ALU.add, ALU.mult)
                last.then_inc(norm[k], 1)

            def key_times_table(b):
                reach(pool, k_copied, b)
                reach(pool, scan_steps, b - 1, 1, 3)
                reach(pool, a_ss, b - 1)
                if b == 0:
                    pool.wait_ge(table_steps, 2)
                pool.tensor_tensor(kw[:], k_sb[:], w_table[:], ALU.mult).then_inc(kw_ready, 1)

            def rms_power(b):
                reach(pool, msq_ready, b)
                reach(pool, x1_ready, b - 1)
                pool.tensor_tensor(rrms[:], msq[:], neg_half[:], ALU.pow).then_inc(rrms_ready, 1)

            def token_difference(k, b):
                reach(pool, xt_ready[k], b)
                reach(pool, mixed[k], b - 1, 2, 2)
                if k == "ffn2" and b >= 1:
                    pool.wait_ge(stored[(b - 1) % 2], 16 * ((b - 1) // 2 + 1))
                pool.tensor_tensor(dx[k][:], xnt[k][:, 1:1 + T], xnt[k][:, 0:T], ALU.subtract)\
                    .then_inc(dx_ready[k], 1)

            def ffn_residual(k, b):
                p = b % 2
                reach(pool, gated_ready[k], b)
                pool.tensor_tensor(DST[k][p][:], gated[k][:].rearrange("p (t d) -> p t d", t=NT),
                                   SRC[k][p][:], ALU.add).then_inc(ffn_out[k], 1)

            def residual_bias(b):
                p = b % 2
                reach(pool, x3_ready, b - 1)
                if b == 0:
                    pool.wait_ge(bias_ready, 1)
                pool.tensor_tensor(x_2b[:], x_2[p][:],
                                   bias_o[:].rearrange("p (o d) -> p o d", o=1).to_broadcast([P, NT, D]),
                                   ALU.add).then_inc(x2b_ready, 1)

            def split_rest(n, b, i):
                reach(pool, cast[n], b, i + 1, 2)
                if i == 0:
                    pool.tensor_tensor(qres[n][:], qf[n][:], parts[n][:, 0, :], ALU.subtract).then_inc(rest[n], 1)
                else:
                    pool.tensor_tensor(parts[n][:, 2, :], qres[n][:], parts[n][:, 1, :], ALU.subtract)\
                        .then_inc(rest[n], 1)

            def mask_diagonal(s, b, g, j):
                reach(pool, exp_done, b, N2 * g + EXPS_OF[j], NG * N2)
                blk = pt[s % 2][:, PT_AT[j]:PT_AT[j] + G * WIDTH[j]].rearrange("p (h q) -> p h q", h=G)[:, :, 0:P]
                pool.affine_select(out=blk, in_=blk, compare_op=ALU.is_ge, fill=0.0, base=0,
                                   pattern=[[0, G], [1, P]], channel_multiplier=-1).then_inc(masked, 1)

            def iteration(b):
                for at, s, g, k in slots(b):
                    for j in range(NT):
                        for slot in due(SLOT_STEP[f"mask {j}"], b, g, k):
                            mask_diagonal(*slot, j)
                    for n in sequence_at("residual bias", POOL_STEP["residual bias"], b, at):
                        residual_bias(n)
                    for n in sequence_at("retention", POOL_STEP["normalise retention"], b, at):
                        normalise("retention", n)
                        if n == 0:
                            attention_biases()
                    for n in sequence_at("retention", POOL_STEP["key times table"], b, at):
                        key_times_table(n)
                    for n in sequence_at("retention", POOL_STEP["rms power"], b, at):
                        rms_power(n)
                    for n in sequence_at("ffn1", POOL_STEP["normalise ffn1"], b, at):
                        normalise("ffn1", n)
                    for n in sequence_at("ffn1", POOL_STEP["token difference ffn1"], b, at):
                        token_difference("ffn1", n)
                    for n in sequence_at("ffn1", POOL_STEP["ffn residual ffn1"], b, at):
                        ffn_residual("ffn1", n)
                    for n in sequence_at("attention", POOL_STEP["normalise attention"], b, at):
                        normalise("attention", n)
                    for n in sequence_at("attention", POOL_STEP["split rest q 0"], b, at):
                        split_rest("q", n, 0)
                    for n in sequence_at("attention", POOL_STEP["split rest q 1"], b, at):
                        split_rest("q", n, 1)
                    for n in sequence_at("attention", POOL_STEP["split rest k 0"], b, at):
                        split_rest("k", n, 0)
                    for n in sequence_at("attention", POOL_STEP["split rest k 1"], b, at):
                        split_rest("k", n, 1)
                    for n in sequence_at("ffn2", POOL_STEP["normalise ffn2"], b, at):
                        normalise("ffn2", n)
                    for n in sequence_at("ffn2", POOL_STEP["token difference ffn2"], b, at):
                        token_difference("ffn2", n)
                    for n in sequence_at("ffn2", POOL_STEP["ffn residual ffn2"], b, at):
                        ffn_residual("ffn2", n)

            pool.wait_ge(fills, 4)
            for b in ITERATIONS:
                iteration(b)

        @block.scalar
        def _(act):
            act.dma_start(bw, w_a).then_inc(bw_in, 16)
            act.dma_start(dcol[:, 0:1], decay).then_inc(table_in, 16)
            act.dma_start(w_table[:], pos).then_inc(table_in, 16)
            act.dma_start(lnw[:], ln_w).then_inc(cols_in, 16)
            act.dma_start(bcol[:], b_cols).then_inc(cols_in, 16)
            act.wait_ge(table_in, 16 * 2)
            act.activation(dcol[:, 1:2], dcol[:, 0:1], ACT.Exp, scale=-1.0).then_inc(decay_steps, 1)
            act.wait_ge(decay_steps, 4)
            act.activation(dcol[:, 4:5], dcol[:, 3:4], ACT.Ln).then_inc(decay_steps, 1)
            act.wait_ge(decay_steps, 5)
            act.activation(w_table[:], w_table[:], ACT.Exp, scale=dcol[:, 4:5]).then_inc(table_steps, 1)

            def copy_turned(k, b):
                reach(act, turned[k], b)
                if k in FF:
                    reach(act, mixed[k], b - 1, 2, 2)
                act.activation(xnt[k][:, 1:1 + T], bank_of(k, b)[:], ACT.Copy).then_inc(xt_ready[k], 1)

            def copy_k(b):
                reach(act, a_k, b)
                reach(act, kw_ready, b - 1)
                act.activation(k_sb[:], bank_of("retention", b)[:], ACT.Copy).then_inc(k_copied, 1)

            def tanh_r(b):
                reach(act, a_r, b)
                reach(act, scan_steps, b - 1, 3, 3)
                act.activation(r_tanh[:], bank_of("retention", b)[:], ACT.Tanh, scale=0.5).then_inc(a_tanh, 1)

            def ffn_tanh(k, b):
                reach(act, f_r[k], b)
                reach(act, gated_ready[k], b - 1)
                act.activation(f_tanh[k][:], bank_of(k, b)[:], ACT.Tanh, scale=0.5).then_inc(f_tanh_ready[k], 1)

            def ffn_relu(k, b):
                reach(act, f_k[k], b)
                reach(act, act_ready[k], b - 1)
                act.activation(k_relu[k][:], bank_of(k, b)[:], ACT.Relu).then_inc(relu_ready[k], 1)

            def square_u(b):
                reach(act, scan_steps, b, 3, 3)
                reach(act, a_ss, b - 1)
                act.activation(usq[:], u[:], ACT.Square).then_inc(usq_ready, 1)

            def square_relu(k, b):
                reach(act, relu_ready[k], b)
                reach(act, f_v[k], b - 1)
                act.activation(k_act[k][:], k_relu[k][:], ACT.Square).then_inc(act_ready[k], 1)

            def project_q(b):
                reach(act, b_q, b)
                reach(act, rest["q"], b - 1, 1, 2)
                if b == 0:
                    act.wait_ge(bq_ready, 1)
                act.activation(qf["q"][:], c_bank[:], ACT.Identity, bias=bq_s[:], scale=float(SCALE))\
                    .then_inc(qf_ready["q"], 1)

            def project_k(b):
                reach(act, b_k, b)
                reach(act, rest["k"], b - 1, 1, 2)
                act.activation(qf["k"][:], c_bank[:], ACT.Identity, bias=bcol[:, 1:2])\
                    .then_inc(qf_ready["k"], 1)

            def exponentials(s, b, g, i):
                j, heads = P2_UNITS[i]
                reach(act, s2_full, b, N2 * g + i + 1, NG * N2)
                if i == 0:
                    reach(act, pv_done, b, NT * (g - 1), NG * NT)
                n = WIDTH[j] * len(heads)
                a = PT_AT[j] + WIDTH[j] * heads[0]
                act.activation(pt[s % 2][:, a:a + n], s2_bank[(g + i) % 2][:, 0:n], ACT.Exp).then_inc(exp_done, 1)

            def copy_o(s, b, g):
                reach(act, pv_done, b, NT * (g + 1), NG * NT)
                reach(act, o_turned, b, g, NG)
                act.activation(o_sb[s % 2][:], o_bank[:], ACT.Copy).then_inc(o_copied, 1)

            def copy_o_t(b):
                reach(act, c_turned, b)
                act.activation(o_t[:], c_bank[:], ACT.Copy).then_inc(ot_ready, 1)

            def iteration(b):
                for at, s, g, k in slots(b):
                    for i in range(N2):
                        for slot in due(SLOT_STEP["second pass"] + i, b, g, k):
                            exponentials(*slot, i)
                    for slot in due(SLOT_STEP["copy o"], b, g, k):
                        copy_o(*slot)
                    for n in sequence_at("retention", ACT_STEP["copy turned retention"], b, at):
                        copy_turned("retention", n)
                    for n in sequence_at("retention", ACT_STEP["copy k"], b, at):
                        copy_k(n)
                    for n in sequence_at("retention", ACT_STEP["tanh r"], b, at):
                        tanh_r(n)
                    for n in sequence_at("retention", ACT_STEP["square u"], b, at):
                        square_u(n)
                    for n in sequence_at("ffn1", ACT_STEP["copy turned ffn1"], b, at):
                        copy_turned("ffn1", n)
                    for n in sequence_at("ffn1", ACT_STEP["ffn tanh ffn1"], b, at):
                        ffn_tanh("ffn1", n)
                    for n in sequence_at("ffn1", ACT_STEP["ffn relu ffn1"], b, at):
                        ffn_relu("ffn1", n)
                    for n in sequence_at("ffn1", ACT_STEP["square relu ffn1"], b, at):
                        square_relu("ffn1", n)
                    for n in sequence_at("attention", ACT_STEP["copy turned attention"], b, at):
                        copy_turned("attention", n)
                    for n in sequence_at("attention", ACT_STEP["project q"], b, at):
                        project_q(n)
                    for n in sequence_at("attention", ACT_STEP["project k"], b, at):
                        project_k(n)
                    for n in sequence_at("ffn2", ACT_STEP["copy o t"], b, at):
                        copy_o_t(n)
                    for n in sequence_at("ffn2", ACT_STEP["copy turned ffn2"], b, at):
                        copy_turned("ffn2", n)
                    for n in sequence_at("ffn2", ACT_STEP["ffn tanh ffn2"], b, at):
                        ffn_tanh("ffn2", n)
                    for n in sequence_at("ffn2", ACT_STEP["ffn relu ffn2"], b, at):
                        ffn_relu("ffn2", n)
                    for n in sequence_at("ffn2", ACT_STEP["square relu ffn2"], b, at):
                        square_relu("ffn2", n)

            for b in ITERATIONS:
                iteration(b)

        @block.vector
        def _(dve):
            dve.memset(v_aug[0][:], 1.0).then_inc(ones_set, 1)

            def statistics(k, b):
                p = b % 2
                wait_source(dve, k, b, p)
                for t in range(NT):
                    last = dve.bn_stats(st[k][:, t, :], SRC[k][p][:, t, :])
                last.then_inc(stats[k], 1)
                reach(dve, stats[k], b, 1, 2)
                reach(dve, norm[k], b - 1, 3, 4)
                for t in range(NT):
                    last = dve.bn_aggr(mv[k][:, t, :], st[k][:, t, :])
                last.then_inc(stats[k], 1)

            def decay_factor():
                dve.wait_ge(decay_steps, 1)
                dve.tensor_scalar(dcol[:, 2:3], dcol[:, 1:2], 1.0, None, ALU.add).then_inc(decay_steps, 1)
                dve.wait_ge(decay_steps, 2)
                dve.reciprocal(dcol[:, 5:6], dcol[:, 2:3]).then_inc(decay_steps, 1)
                dve.wait_ge(decay_steps, 3)
                dve.tensor_scalar(dcol[:, 3:4], dcol[:, 5:6], 1e-7, None, ALU.max).then_inc(decay_steps, 1)

            def ternary_weights():
                dve.wait_ge(bw_in, 16)
                dve.tensor_reduce(bsum[:], bw, AX.X, ALU.add, apply_absolute_value=True).then_inc(bw_steps, 1)
                dve.wait_ge(bw_steps, 1)
                dve.tensor_scalar(bscale[:], bsum[:], 1.0 / D, 1e-5, ALU.mult, ALU.max).then_inc(bw_steps, 1)
                dve.wait_ge(bw_steps, 2)
                dve.tensor_scalar(bhalf[:, 0, :], bscale[:], 0.5, None, ALU.mult)
                dve.tensor_scalar(bhalf[:, 1, :], bscale[:], -0.5, None, ALU.mult).then_inc(bw_steps, 1)
                dve.wait_ge(bw_steps, 3)
                for i in range(4):
                    dve.tensor_scalar(bw_gt[:, i, :], bw[:, i, :], bhalf[:, 0, i:i + 1], bscale[:, i:i + 1],
                                      ALU.is_gt, ALU.mult)
                    last = dve.tensor_scalar(bw_lt[:, i, :], bw[:, i, :], bhalf[:, 1, i:i + 1], bscale[:, i:i + 1],
                                             ALU.is_lt, ALU.mult)
                last.then_inc(bw_steps, 1)
                decay_factor()
                dve.wait_ge(bw_steps, 4)
                dve.tensor_tensor(bw_q, bw_gt, bw_lt, ALU.subtract).then_inc(bw_steps, 1)
                dve.wait_ge(bw_steps, 5)
                dve.tensor_tensor(bw_gt, bw_q, bw, ALU.subtract).then_inc(bw_steps, 1)
                dve.wait_ge(bw_steps, 6)
                dve.tensor_tensor(bw_q, bw, bw_gt, ALU.add).then_inc(bw_steps, 1)

            def turned_weights():
                dve.wait_ge(bw_turned, 1)
                dve.wait_ge(cols_in, 16 * 4)
                dve.tensor_copy(wa[:, 0:3, :], s2_bank[0][:, 0:3 * P].rearrange("p (w d) -> p w d", w=3))\
                    .then_inc(wa_ready, 1)
                dve.tensor_scalar(wa[:, 3, :], s2_bank[0][:, 3 * P:4 * P], lnw[:, 0:1], None, ALU.mult)\
                    .then_inc(wa_ready, 1)

            def position_table():
                dve.wait_ge(table_steps, 1)
                dve.tensor_scalar(w_table[:], w_table[:], 1.0 / CLIP_SCALE, 1.0, ALU.mult, ALU.min)\
                    .then_inc(table_steps, 1)

            def late_set_up():
                dve.wait_ge(weights_in, 16 * 2)
                dve.tensor_scalar(wf[:, 2, :], wf[:, 2, :], 0.5, None, ALU.mult).then_inc(wf_ready, 1)
                dve.wait_ge(bias_product, 1)
                dve.tensor_tensor(bias_o[:], s2_bank[1][:, 0:D], bo_b[:], ALU.add).then_inc(bias_ready, 1)

            def scan_state(b):
                reach(dve, a_v, b)
                reach(dve, kw_ready, b)
                dve.tensor_tensor(kvw[:], bank_of("retention", b)[:], kw[:], ALU.mult).then_inc(scan_steps, 1)
                reach(dve, scan_steps, b, 1, 3)
                dve.tensor_tensor_scan(state[:], dcol[:, 3:4].to_broadcast([P, T]), kvw[:], 0.0, ALU.mult, ALU.add)\
                    .then_inc(scan_steps, 1)

            def gate_state(b):
                reach(dve, a_tanh, b)
                reach(dve, scan_steps, b, 2, 3)
                reach(dve, a_y, b - 1)
                dve.scalar_tensor_tensor(out=u[:], in0=r_tanh[:], scalar=1.0, in1=state[:],
                                         op0=ALU.add, op1=ALU.mult).then_inc(scan_steps, 1)

            def mean_square(b):
                reach(dve, a_ss, b)
                reach(dve, rrms_ready, b - 1)
                dve.tensor_scalar(msq[:], bank_of("retention", b)[:, 0:NT], 1.0 / D, 4.0 * RMS_EPS, ALU.mult, ALU.add)\
                    .then_inc(msq_ready, 1)

            def retention_residual(b):
                p = b % 2
                reach(dve, a_y, b)
                reach(dve, rrms_ready, b)
                reach(dve, ffn_out["ffn1"], b - 1)
                for t in range(NT):
                    last = dve.scalar_tensor_tensor(out=x_1[p][:, t, :],
                                                    in0=bank_of("retention", b)[:, t * P:(t + 1) * P],
                                                    scalar=rrms[:, t:t + 1], in1=x_in[p][:, t, :],
                                                    op0=ALU.mult, op1=ALU.add)
                last.then_inc(x1_ready, 1)

            def mix(k, b):
                reach(dve, dx_ready[k], b)
                reach(dve, f_k[k], b - 1)
                if k == "ffn2":
                    reach(dve, c_y, b)
                for i, dst in enumerate((xr[k], xk[k])):
                    dve.scalar_tensor_tensor(out=dst[:], in0=dx[k][:], scalar=mu_sb[:, i:i + 1],
                                             in1=xnt[k][:, 0:T], op0=ALU.mult, op1=ALU.add).then_inc(mixed[k], 1)

            def gate_ffn(k, b):
                reach(dve, f_v[k], b)
                reach(dve, f_tanh_ready[k], b)
                reach(dve, ffn_out[k], b - 1)
                dve.scalar_tensor_tensor(out=gated[k][:], in0=f_tanh[k][:], scalar=1.0, in1=bank_of(k, b)[:],
                                         op0=ALU.add, op1=ALU.mult).then_inc(gated_ready[k], 1)

            def cast_part(n, b, i):
                if i == 0:
                    reach(dve, qf_ready[n], b)
                    if b:
                        dve.wait_ge(parts_out[(b - 1) % 2], 96 * ((b - 1) // 2 + 1))
                    dve.tensor_copy(parts[n][:, 0, :], qf[n][:]).then_inc(cast[n], 1)
                else:
                    reach(dve, rest[n], b, 1, 2)
                    dve.tensor_copy(parts[n][:, 1, :], qres[n][:]).then_inc(cast[n], 1)

            def copy_v(b):
                p = b % 2
                reach(dve, b_v, b)
                reach(dve, pv_done, b - 2, NG * NT, NG * NT)
                if b < 2:
                    dve.wait_ge(ones_set, 2)
                dve.tensor_copy(v_aug[p][:, :, :, 0:HD], c_bank[:].rearrange("p (t h d) -> p t h d", t=NT, h=H))\
                    .then_inc(v_ready, 1)

            def block_maxima(b, g, i):
                nxt = (g + 1) % 2
                unit = P1_UNITS[i]
                h, q = unit[0]
                bank = s1_of(b, g, i)
                reach(dve, s1_full, b, s1_at(b, g, i) + 1, NG * N1)
                if i == 0:
                    reach(dve, mparts_ready, b, 2 * g, 2 * NG)
                if q == 3:
                    dve.tensor_reduce(negm[nxt][:, h, 3:4], bank[:], AX.X, ALU.max, negate=True).then_inc(s1_free, 1)
                elif q == 1:
                    dve.tensor_reduce(negm[nxt][:, h:h + 2, 1:2].rearrange("p h o -> p (h o)"),
                                      bank[:].rearrange("p (h k) -> p h k", h=2),
                                      AX.X, ALU.max, negate=True).then_inc(s1_free, 1)
                else:
                    dve.tensor_reduce(bmax[nxt][:, h, :], bank[:].rearrange("p (j k) -> p j k", j=NT),
                                      AX.X, ALU.max).then_inc(s1_free, 1)

            def group_maxima(b, g):
                nxt = (g + 1) % 2
                reach(dve, s1_free, b, s1_at(b, g, N1 - 2) + 1, NG * N1)
                dve.tensor_reduce(negm[nxt][:, :, 2:3].rearrange("p h o -> p (h o)"), bmax[nxt][:, :, 0:3],
                                  AX.X, ALU.max, negate=True).then_inc(negm_ready, 1)
                dve.tensor_scalar(negm[nxt][:, :, 0], bmax[nxt][:, :, 3], -1.0, None, ALU.mult)\
                    .then_inc(negm_ready, 1)

            def split_max(s, b, g):
                p = s % 2
                reach(dve, negm_ready, b, 2 * g + 2, 2 * NG)
                dve.tensor_copy(m_parts[p][:, 0, :], negm[p][:].rearrange("p h i -> p (h i)"))\
                    .then_inc(mparts_ready, 1)
                reach(dve, mparts_ready, b, 2 * g + 1, 2 * NG)
                dve.tensor_tensor(m_parts[p][:, 1, :], negm[p][:].rearrange("p h i -> p (h i)"),
                                   m_parts[p][:, 0, :], ALU.subtract).then_inc(mparts_ready, 1)

            def copy_max_rows(s, b, g):
                p = s % 2
                reach(dve, s1_full, b, s1_at(b, g) + 1, NG * N1)
                if s >= 2:
                    dve.wait_ge(m_loaded[p], 32 * (s // 2))
                dve.tensor_copy(m_rows[p][:], s1_of(b, g)[0:2 * G * NT, 0:P // 2].bitcast(BF16))\
                    .then_inc(s1_free, 1)

            def normalise_o(s, b, g):
                reach(dve, o_turned, b, g + 1, NG)
                o = o_bank[:].rearrange("p (t h c) -> p t h c", t=NT, h=G)
                dve.reciprocal(rsum[:], o[:, :, :, HD]).then_inc(o_normed, 1)
                reach(dve, o_normed, b, 2 * g + 1, 2 * NG)
                if g == 0:
                    reach(dve, c_turned, b - 1)
                dst = o_tm[(s // NG) % 2][:, :, G * HD * g:G * HD * (g + 1)].rearrange("p t (h d) -> p t h d", h=G)
                dve.tensor_tensor(dst, o[:, :, :, 0:HD],
                                  rsum[:].rearrange("p t (h o) -> p t h o", o=1).to_broadcast([P, NT, G, HD]),
                                  ALU.mult).then_inc(o_normed, 1)

            def attention_residual(b):
                p = b % 2
                reach(dve, c_y, b)
                reach(dve, x2b_ready, b)
                dve.tensor_tensor(x_3[p][:].rearrange("p t d -> p (t d)"), c_bank[:],
                                  x_2b[:].rearrange("p t d -> p (t d)"), ALU.add).then_inc(x3_ready, 1)

            def iteration(b):
                for at, s, g, k in slots(b):
                    for slot in due(SLOT_STEP["normalise o"], b, g, k):
                        normalise_o(*slot)
                    if k < TURN_AT and live(s + 1):
                        block_maxima(b, g, k)
                    if k == 0 and live(s):
                        split_max(s, b, g)
                    if k == TURN_AT and live(s):
                        copy_max_rows(s, b, g)
                    if k > TURN_AT and live(s + 1):
                        block_maxima(b, g, k - 1)
                        if k == STEPS - 1:
                            group_maxima(b, g)
                    for n in sequence_at("retention", DVE_STEP["statistics retention"], b, at):
                        if n:
                            statistics("retention", n)
                    for n in sequence_at("retention", DVE_STEP["scan state"], b, at):
                        scan_state(n)
                    for n in sequence_at("retention", DVE_STEP["gate state"], b, at):
                        gate_state(n)
                    for n in sequence_at("retention", DVE_STEP["mean square"], b, at):
                        mean_square(n)
                    for n in sequence_at("retention", DVE_STEP["retention residual"], b, at):
                        retention_residual(n)
                        statistics("ffn1", n)
                    for n in sequence_at("ffn1", DVE_STEP["mix ffn1"], b, at):
                        mix("ffn1", n)
                        if n == 0:
                            late_set_up()
                    for n in sequence_at("ffn1", DVE_STEP["gate ffn ffn1"], b, at):
                        gate_ffn("ffn1", n)
                    for n in sequence_at("attention", DVE_STEP["statistics attention"], b, at):
                        statistics("attention", n)
                    for n in sequence_at("attention", DVE_STEP["cast part q 0"], b, at):
                        cast_part("q", n, 0)
                    for n in sequence_at("attention", DVE_STEP["copy v"], b, at):
                        copy_v(n)
                    for n in sequence_at("attention", DVE_STEP["cast part k 0"], b, at):
                        cast_part("k", n, 0)
                    for n in sequence_at("attention", DVE_STEP["cast part q 1"], b, at):
                        cast_part("q", n, 1)
                    for n in sequence_at("attention", DVE_STEP["cast part k 1"], b, at):
                        cast_part("k", n, 1)
                    for n in sequence_at("ffn2", DVE_STEP["attention residual"], b, at):
                        attention_residual(n)
                        statistics("ffn2", n)
                    for n in sequence_at("ffn2", DVE_STEP["mix ffn2"], b, at):
                        mix("ffn2", n)
                    for n in sequence_at("ffn2", DVE_STEP["gate ffn ffn2"], b, at):
                        gate_ffn("ffn2", n)

            statistics("retention", 0)
            ternary_weights()
            turned_weights()
            position_table()
            for b in ITERATIONS:
                iteration(b)

        @block.tensor
        def _(pe):
            def turn_weights():
                pe.wait_ge(bw_steps, 7)
                for i in range(4):
                    last = pe.transpose(s2_bank[0][:, i * P:(i + 1) * P], bw_q[:, i, :], id_f[:])
                last.then_inc(bw_turned, 1)

            def bias_through_weights():
                pe.wait_ge(bv_ready, 1)
                pe.wait_ge(weights_in, 16 * 2)
                pe.matmul(s2_bank[1][:, 0:D], bv_b[:], wb[:, 3, :], start=True, stop=True).then_inc(bias_product, 1)

            def turn(k, b):
                reach(pe, norm[k], b, 4, 4)
                if k == "attention":
                    reach(pe, gated_ready["ffn2"], b - 3)
                    if b == 0:
                        pe.wait_ge(x1_ready, 2)
                elif k == "ffn2":
                    reach(pe, x3_ready, b)
                elif k == "ffn1" or b != 1:
                    reach(pe, gated_ready["ffn1"], b - 1)
                for t in range(NT):
                    last = pe.transpose(bank_of(k, b)[:, t * P:(t + 1) * P], xn[k][:, t, :], id_f[:])
                last.then_inc(turned[k], 1)

            def to_channels(bank, weight, src, signal):
                pe.matmul(bank[:], weight, src, start=True, stop=True).then_inc(signal, 1)

            def to_tokens(bank, src, weight, signal):
                for t in range(NT):
                    last = pe.matmul(bank[:, t * P:(t + 1) * P], src[:, t * P:(t + 1) * P], weight,
                                     start=True, stop=True)
                last.then_inc(signal, 1)

            def retention_k(b):
                reach(pe, xt_ready["retention"], b)
                if b == 0:
                    pe.wait_ge(wa_ready, 2)
                to_channels(bank_of("retention", b), wa[:, 1, :], xnt["retention"][:, 1:1 + T], a_k)

            def retention_r(b):
                reach(pe, k_copied, b)
                to_channels(bank_of("retention", b), wa[:, 0, :], xnt["retention"][:, 1:1 + T], a_r)

            def retention_v(b):
                reach(pe, a_tanh, b)
                to_channels(bank_of("retention", b), wa[:, 2, :], xnt["retention"][:, 1:1 + T], a_v)

            def sum_squares(b):
                reach(pe, usq_ready, b)
                reach(pe, scan_steps, b, 1, 3)
                for t in range(NT):
                    last = pe.matmul(bank_of("retention", b)[:, t:t + 1], usq[:, t * P:(t + 1) * P], ones_f[:, 0:1],
                                     start=True, stop=True)
                last.then_inc(a_ss, 1)

            def retention_out(b):
                reach(pe, msq_ready, b)
                reach(pe, scan_steps, b, 3, 3)
                to_tokens(bank_of("retention", b), u, wa[:, 3, :], a_y)

            def ffn_r(k, b):
                reach(pe, mixed[k], b, 1, 2)
                to_tokens(bank_of(k, b), xr[k], wf[:, 0, :], f_r[k])

            def ffn_k(k, b):
                reach(pe, mixed[k], b, 2, 2)
                reach(pe, f_tanh_ready[k], b)
                to_channels(bank_of(k, b), wf[:, 1, :], xk[k][:], f_k[k])

            def ffn_v(k, b):
                reach(pe, act_ready[k], b)
                if b == 0:
                    pe.wait_ge(wf_ready, 1)
                to_tokens(bank_of(k, b), k_act[k], wf[:, 2, :], f_v[k])

            def attention_q(b):
                reach(pe, xt_ready["attention"], b)
                to_channels(c_bank, wb[:, 0, :], xnt["attention"][:, 1:1 + T], b_q)

            def attention_k(b):
                reach(pe, qf_ready["q"], b)
                to_channels(c_bank, wb[:, 1, :], xnt["attention"][:, 1:1 + T], b_k)

            def attention_v(b):
                reach(pe, qf_ready["k"], b)
                to_tokens(c_bank, xnt["attention"][:, 1:1 + T], wb[:, 2, :], b_v)

            def first_pass(b, g, i):
                nb, ng = (b, g + 1) if g + 1 < NG else (b + 1, 0)
                p = nb % 2
                if ng == 0 and i == 0:
                    pe.wait_ge(aug_loaded[p], 16 * 9 * (nb // 2 + 1))
                    if nb < 2:
                        pe.wait_ge(aug_in, 16 * 8)
                        pe.wait_ge(masks_in, 16 * 2)
                bank = s1_of(b, g, i)
                reach(pe, s1_free, b, s1_at(b, g, i) - 2, NG * N1)
                col = 0
                for h, q in P1_UNITS[i]:
                    n = P * (q + 1)
                    head = G * ng + h
                    pe.matmul(bank[:, col:col + n], q_aug[p][0:MROW, head, q * P:(q + 1) * P],
                              k_aug[p][0:MROW, head, 0:n], start=(col == 0), stop=False)
                    col += n
                if q == 3:
                    diagonals, mask = bank[:, T - P:T], mask_b[:]
                else:
                    blocks = bank[:].rearrange("p (j k) -> p j k", j=NT)
                    diagonals = blocks[:, 2:4] if q == 0 else blocks[:, 1:4:2]
                    mask = mask_b[:].rearrange("p (o k) -> p o k", o=1).to_broadcast([P, 2, P])
                pe.matmul(diagonals, id_b[:], mask, start=False, stop=True).then_inc(s1_full, 1)

            def turn_maxima(s, b, g):
                reach(pe, mparts_ready, b, 2 * g + 2, 2 * NG)
                reach(pe, s1_free, b, s1_at(b, g) - 2, NG * N1)
                pe.transpose(s1_of(b, g)[0:2 * G * NT, 0:P // 2].bitcast(BF16),
                             m_parts[s % 2][:].rearrange("p a m -> p (a m)"), id_b[:]).then_inc(s1_full, 1)

            def second_pass(s, b, g, i):
                j, heads = P2_UNITS[i]
                p = (s // NG) % 2
                if i == 0:
                    pe.wait_ge(m_loaded[s % 2], 32 * (s // 2 + 1))
                reach(pe, exp_done, b, N2 * g + i - 1, NG * N2)
                w = WIDTH[j]
                for c, h in enumerate(heads):
                    last = pe.matmul(s2_bank[(g + i) % 2][:, c * w:(c + 1) * w],
                                     k_aug[p][0:KROWS, G * g + h, j * P:(j + 1) * P],
                                     q_aug[p][0:KROWS, G * g + h, j * P:T], start=True, stop=True)
                last.then_inc(s2_full, 1)

            def weigh_values(s, b, g, j):
                p = (s // NG) % 2
                reach(pe, masked, b, NT * g + j + 1, NG * NT)
                if j == 0:
                    reach(pe, o_normed, b, 2 * g, 2 * NG)
                    if g == 0:
                        reach(pe, v_ready, b)
                w = WIDTH[j]
                for h in range(G):
                    a = PT_AT[j] + w * h
                    last = pe.matmul(o_bank[VW * h:VW * (h + 1), j * P:T], v_aug[p][:, j, G * g + h, :],
                                     pt[s % 2][:, a:a + w], start=(j == 0), stop=(j == NT - 1))
                last.then_inc(pv_done, 1)

            def turn_o(s, b, g):
                reach(pe, o_copied, b, g + 1, NG)
                for t in range(NT):
                    last = pe.transpose(o_bank[:, t * P:(t + 1) * P], o_sb[s % 2][:, t * P:(t + 1) * P], id_f[:])
                last.then_inc(o_turned, 1)

            def turn_heads(b):
                reach(pe, o_normed, b, 2 * NG, 2 * NG)
                reach(pe, gated_ready["ffn2"], b - 1)
                reach(pe, v_ready, min(b + 2, B - 1))
                for t in range(NT):
                    last = pe.transpose(c_bank[:, t * P:(t + 1) * P], o_tm[b % 2][:, t, :], id_f[:])
                last.then_inc(c_turned, 1)

            def attention_out(b):
                reach(pe, ot_ready, b)
                to_tokens(c_bank, o_t, wb[:, 3, :], c_y)

            pe.wait_ge(ident_in, 16)

            def iteration(b):
                for at, s, g, k in slots(b):
                    if k == TURN_AT and live(s):
                        turn_maxima(s, b, g)
                    elif k != TURN_AT and live(s + 1):
                        first_pass(b, g, k if k < TURN_AT else k - 1)
                    for i in range(N2):
                        for slot in due(SLOT_STEP["second pass"] + i, b, g, k):
                            second_pass(*slot, i)
                    for j in range(NT):
                        for slot in due(SLOT_STEP[f"weigh values {j}"], b, g, k):
                            weigh_values(*slot, j)
                    for slot in due(SLOT_STEP["turn o"], b, g, k):
                        turn_o(*slot)
                    for n in sequence_at("retention", PE_STEP["turn retention"], b, at):
                        turn("retention", n)
                        if n == 0:
                            turn_weights()
                    for n in sequence_at("retention", PE_STEP["retention k"], b, at):
                        retention_k(n)
                    for n in sequence_at("retention", PE_STEP["retention r"], b, at):
                        retention_r(n)
                    for n in sequence_at("retention", PE_STEP["retention v"], b, at):
                        retention_v(n)
                    for n in sequence_at("retention", PE_STEP["sum squares"], b, at):
                        sum_squares(n)
                    for n in sequence_at("retention", PE_STEP["retention out"], b, at):
                        retention_out(n)
                    for n in sequence_at("ffn1", PE_STEP["turn ffn1"], b, at):
                        turn("ffn1", n)
                        if n == 0:
                            bias_through_weights()
                    for n in sequence_at("ffn1", PE_STEP["ffn r ffn1"], b, at):
                        ffn_r("ffn1", n)
                    for n in sequence_at("ffn1", PE_STEP["ffn k ffn1"], b, at):
                        ffn_k("ffn1", n)
                    for n in sequence_at("ffn1", PE_STEP["ffn v ffn1"], b, at):
                        ffn_v("ffn1", n)
                    for n in sequence_at("attention", PE_STEP["turn attention"], b, at):
                        turn("attention", n)
                    for n in sequence_at("attention", PE_STEP["attention q"], b, at):
                        attention_q(n)
                    for n in sequence_at("attention", PE_STEP["attention k"], b, at):
                        attention_k(n)
                    for n in sequence_at("attention", PE_STEP["attention v"], b, at):
                        attention_v(n)
                    for n in sequence_at("ffn2", PE_STEP["turn heads"], b, at):
                        turn_heads(n)
                    for n in sequence_at("ffn2", PE_STEP["attention out"], b, at):
                        attention_out(n)
                    for n in sequence_at("ffn2", PE_STEP["turn ffn2"], b, at):
                        turn("ffn2", n)
                    for n in sequence_at("ffn2", PE_STEP["ffn r ffn2"], b, at):
                        ffn_r("ffn2", n)
                    for n in sequence_at("ffn2", PE_STEP["ffn k ffn2"], b, at):
                        ffn_k("ffn2", n)
                    for n in sequence_at("ffn2", PE_STEP["ffn v ffn2"], b, at):
                        ffn_v("ffn2", n)

            for b in ITERATIONS:
                iteration(b)


def bf16_parts(a, n):
    out = []
    for _ in range(n):
        part = a.astype(mybir.dt.np(BF16))
        out.append(part)
        a = (a - part.astype(np.float32)).astype(np.float32)
    return out


def constants():
    bf = mybir.dt.np(BF16)
    slope = np.power(np.float32(2.0), (-8.0 * np.arange(1, H + 1) / H).astype(np.float32)).astype(np.float32)
    token = np.arange(T)
    lo, hi = (token % 256).astype(bf), (token - token % 256).astype(bf)
    aug_q = np.zeros((KROWS - NSPLIT, H, T), bf)
    aug_k = np.zeros((KROWS - NSPLIT, H, T), bf)
    aug_k[MROW - NSPLIT:] = 1.0
    for i, s in enumerate(bf16_parts(slope, 3)):
        aug_q[4 * i] = aug_q[4 * i + 1] = s[:, None]
        aug_k[4 * i], aug_k[4 * i + 1] = lo, hi
        aug_q[4 * i + 2], aug_q[4 * i + 3] = lo, hi
        aug_k[4 * i + 2] = aug_k[4 * i + 3] = -s[:, None]
    for r in range(1, T // SUB):
        aug_k[NBIAS + r - 1] = (token // SUB == r).astype(bf)
        aug_q[NBIAS + r - 1] = np.where(token // SUB < r, np.float32(FAR), np.float32(0)).astype(bf)
    causal = np.where(np.arange(P)[None, :] > np.arange(P)[:, None], np.float32(FAR), np.float32(0)).astype(bf)
    return {
        "ident": np.eye(P, dtype=np.float32), "ident_b": np.eye(P, dtype=np.float32).astype(bf), "causal": causal,
        "pos": np.broadcast_to(np.arange(T, dtype=np.float32), (P, T)).copy(), "aug_q": aug_q, "aug_k": aug_k,
    }


def kernel(**inputs):
    import concourse.bacc as _bacc
    from concourse.bass_utils import run_bass_kernel_spmd as _run

    a = {k: np.asarray(v) for k, v in inputs.items()}

    def col(*names):
        return np.ascontiguousarray(np.stack([a[n] for n in names], axis=1))

    arrays = {
        "x": np.ascontiguousarray(a["L0_attn_a_x"]),
        "w_a": np.ascontiguousarray(np.stack([a[f"L0_attn_a_W{n}"] for n in "rkvo"], axis=1)),
        "w_f": np.ascontiguousarray(np.stack([a[f"L0_ffn_W_{n}"].T for n in "rkv"], axis=1)),
        "w_b": np.ascontiguousarray(np.stack([a[f"L0_attn_b_W{n}"].T for n in "qkvo"], axis=1)),
        "decay": col("L0_attn_a_decay"), "ln_w": col("L0_attn_a_ln_w"),
        "mu": col("L0_ffn_mu_r", "L0_ffn_mu_k"),
        "b_cols": col("L0_attn_b_bq", "L0_attn_b_bk", "L0_attn_b_bv"),
        "bo_row": np.ascontiguousarray(a["L0_attn_b_bo"].reshape(1, D)),
        **constants(),
    }
    nc = _bacc.Bacc("TRN2", target_bir_lowering=False, num_devices=1)
    args = {k: nc.dram_tensor(k, v.shape, mybir.dt.from_np(v.dtype), kind="ExternalInput").ap()
            for k, v in arrays.items()}
    args["out"] = nc.dram_tensor("out", (B, T, D), F32, kind="ExternalOutput").ap()
    build(nc, **args)
    r = _run(nc, [arrays], core_ids=[0])
    return r.results[0]["out"]
```
